# Optimizing a Trainium2 kernel written in Bass

```python
import numpy as np
import jax
import jax.numpy as jnp

def _softmax(x, axis=-1):
    return jax.nn.softmax(x, axis=axis)

def _gelu(x):
    return jax.nn.gelu(x, approximate=True)

def _silu(x):
    return jax.nn.silu(x)

def _sigmoid(x):
    return jax.nn.sigmoid(x)

def _layernorm(x, axis=-1, eps=1e-05):
    m = jnp.mean(x, axis=axis, keepdims=True)
    v = jnp.var(x, axis=axis, keepdims=True)
    return (x - m) / jnp.sqrt(v + eps)

def _scatter_add(tgt, idx, src, axis=0):
    return tgt.at[idx].add(src)

def _segment_sum(src, seg, n):
    return jax.ops.segment_sum(src, seg, n)
kernel_name = 'mk_gnn_preln_d1_gnn_r8_6127d9'

def setup_inputs(seed: int=0):
    np.random.seed(seed)
    _w = jnp.asarray

    def _rec_inputs():
        import jax
        import jax.numpy as jnp
        _gk = jax.random.key(seed)
        x = 3.059e-06 + 0.006317 * jax.random.normal(jax.random.fold_in(_gk, 1), (6250, 128), jnp.float32)
        _s = jax.random.randint(jax.random.fold_in(_gk, 2), (50000,), 0, 6250, jnp.int32)
        _d = jax.random.randint(jax.random.fold_in(_gk, 3), (50000,), 0, 6250, jnp.int32)
        _loop = jnp.arange(6250, dtype=jnp.int32)
        src = jnp.concatenate([_s, _d, _loop])
        dst = jnp.concatenate([_d, _s, _loop])
        _o = jnp.argsort(dst, stable=True)
        src = src[_o]
        dst = dst[_o]
        edge_type_16 = jax.random.randint(jax.random.fold_in(_gk, 12), (106250,), 0, 16, jnp.int32)
        return (x, src, dst, edge_type_16)
    x, src, dst, edge_type_16 = _rec_inputs()

    def _L0_gnn_setup():
        import jax, jax.numpy as jnp
        import numpy as np
        N_NODES = 6250
        N_REL = 16
        D_EMB = 128
        D_HID = 128
        D_OUT = 128
        N_EDGES = 200000

        def _xavier(key, shape, fan_in, fan_out, dtype=jnp.float32):
            lim = float(np.sqrt(6.0 / (fan_in + fan_out)))
            return jax.random.uniform(key, shape, dtype, -lim, lim)

        def rgcn_conv(x, edge_index, edge_type, W, W_root, b):
            src, dst = (edge_index[0], edge_index[1])
            seg = dst * N_REL + edge_type
            x_src = x[src]
            summed = jax.ops.segment_sum(x_src, seg, num_segments=N_NODES * N_REL)
            cnt = jax.ops.segment_sum(jnp.ones((src.shape[0],), x.dtype), seg, num_segments=N_NODES * N_REL)
            agg = summed / jnp.maximum(cnt, 1.0)[:, None]
            agg = agg.reshape(N_NODES, N_REL, x.shape[1])
            return jnp.einsum('nrd,rdh->nh', agg, W) + x @ W_root + b
        key = jax.random.key(seed)
        ks = jax.random.split(key, 10)
        edge_index = jax.random.randint(ks[0], (2, N_EDGES), 0, N_NODES, dtype=jnp.int64)
        edge_type = jax.random.randint(ks[1], (N_EDGES,), 0, N_REL, dtype=jnp.int64)
        emb = _xavier(ks[2], (N_NODES, D_EMB), N_NODES, D_EMB)
        W1 = _xavier(ks[3], (N_REL, D_EMB, D_HID), D_EMB, D_HID)
        root1 = _xavier(ks[4], (D_EMB, D_HID), D_EMB, D_HID)
        b1 = jnp.zeros((D_HID,), jnp.float32)
        W2 = _xavier(ks[5], (N_REL, D_HID, D_OUT), D_HID, D_OUT)
        root2 = _xavier(ks[6], (D_HID, D_OUT), D_HID, D_OUT)
        b2 = jnp.zeros((D_OUT,), jnp.float32)
        return {'edge_index': edge_index, 'edge_type': edge_type, 'emb': emb, 'W1': W1, 'root1': root1, 'b1': b1, 'W2': W2, 'root2': root2, 'b2': b2}
    _L0_gnn_all = _L0_gnn_setup()
    _L0_gnn_in = {k: v for k, v in _L0_gnn_all.items() if k in ('W1', 'root1', 'b1', 'W2', 'root2', 'b2')}
    del _L0_gnn_all
    return {'x': x, 'src': src, 'dst': dst, 'edge_type_16': edge_type_16, 'L0_gnn_W1': _L0_gnn_in['W1'], 'L0_gnn_root1': _L0_gnn_in['root1'], 'L0_gnn_b1': _L0_gnn_in['b1'], 'L0_gnn_W2': _L0_gnn_in['W2'], 'L0_gnn_root2': _L0_gnn_in['root2'], 'L0_gnn_b2': _L0_gnn_in['b2']}

def reference(x, src, dst, edge_type_16, L0_gnn_W1, L0_gnn_root1, L0_gnn_b1, L0_gnn_W2, L0_gnn_root2, L0_gnn_b2):
    import jax
    import jax.numpy as jnp

    def _L0_gnn_ref(edge_index, edge_type, emb, W1, root1, b1, W2, root2, b2):
        import jax, jax.numpy as jnp
        import numpy as np
        N_NODES = 6250
        N_REL = 16
        D_EMB = 128
        D_HID = 128
        D_OUT = 128
        N_EDGES = 200000

        def _xavier(key, shape, fan_in, fan_out, dtype=jnp.float32):
            lim = float(np.sqrt(6.0 / (fan_in + fan_out)))
            return jax.random.uniform(key, shape, dtype, -lim, lim)

        def rgcn_conv(x, edge_index, edge_type, W, W_root, b):
            src, dst = (edge_index[0], edge_index[1])
            seg = dst * N_REL + edge_type
            x_src = x[src]
            summed = jax.ops.segment_sum(x_src, seg, num_segments=N_NODES * N_REL)
            cnt = jax.ops.segment_sum(jnp.ones((src.shape[0],), x.dtype), seg, num_segments=N_NODES * N_REL)
            agg = summed / jnp.maximum(cnt, 1.0)[:, None]
            agg = agg.reshape(N_NODES, N_REL, x.shape[1])
            return jnp.einsum('nrd,rdh->nh', agg, W) + x @ W_root + b
        x = emb
        x = jax.nn.relu(rgcn_conv(x, edge_index, edge_type, W1, root1, b1))
        x = rgcn_conv(x, edge_index, edge_type, W2, root2, b2)
        return x
    edge_index = jnp.stack([src, dst])
    h = jnp.maximum(_layernorm(x, axis=-1), 0.0)
    x = x + _L0_gnn_ref(edge_index, edge_type_16, h, L0_gnn_W1, L0_gnn_root1, L0_gnn_b1, L0_gnn_W2, L0_gnn_root2, L0_gnn_b2)
    return x

_drawn_inputs = setup_inputs


def setup_inputs(seed=0):
    import zlib

    import numpy as np

    out = dict(_drawn_inputs(seed))
    spreads = {'L0_gnn_b1': (0.0, 0.1), 'L0_gnn_b2': (0.0, 0.361)}
    factors = {}
    for name, (base, spread) in spreads.items():
        noise = np.random.default_rng([zlib.crc32(name.encode()), seed]).standard_normal(out[name].shape)
        drawn = base * np.exp(spread * noise) if base else spread * noise
        out[name] = jnp.asarray(drawn.astype(out[name].dtype))
    for name, factor in factors.items():
        out[name] = (out[name] * factor).astype(out[name].dtype)
    return out
```

```python
from contextlib import ExitStack

import concourse.bass as bass
from concourse import mybir

F32 = mybir.dt.float32
BF16 = mybir.dt.bfloat16
I32 = mybir.dt.int32
ALU = mybir.AluOpType
ACT = mybir.ActivationFunctionType
AX = mybir.AxisListType
ds = bass.ds

P = 128
EPS = 1e-5
G = 16
RING = 4
WIN = 12
QUAD = 4
QWIN = 48
Z_BANKS = 4
SEED = 1
RELP = 32
BANK = 512


def rgcn_kernel(nc, x, src, dst, rel, w1, root1, b1, w2, root2, b2, out):
    N, D = x.shape
    E = src.shape[0]
    R = w1.shape[0]
    NT = -(-E // (P * G * RING)) * G * RING
    NG = NT // G
    NI = NG // RING
    CH = -(-NT // P)
    FULL = E // P
    LAST = E - FULL * P
    NP = next(p for p in range(P, 0, -1) if N % p == 0)
    NJ = N // NP
    MAXR = -(-N // WIN)
    COLS = N + WIN + (-(N + WIN)) % 4
    QCOLS = N + QWIN + (-(N + QWIN)) % 4
    QG = G // QUAD
    assert D == P and R <= RELP and FULL // P == CH - 1 and 0 < LAST < P and NT - FULL <= 2
    LNC = 10
    NLN = NJ // LNC
    assert NJ % LNC == 0
    JQ = -(-NJ // 4)
    NCH = -(-N // BANK)

    table1 = nc.dram_tensor("h_rows_dram", (N, D), F32).ap()
    table2 = nc.dram_tensor("h1_rows_dram", (N, D), F32).ap()
    rows_of = lambda a: a.rearrange("(p j) d -> p j d", j=NJ)

    with ExitStack() as ctx:
        def sb(name, shape, dt=F32):
            return ctx.enter_context(nc.sbuf_tensor(name, shape, dt))

        def sem(name):
            return ctx.enter_context(nc.semaphore(name))

        ps = ctx.enter_context(nc.psum_tensor("ps", [P, 8 * BANK], F32))
        Z_BANK, REL_BANK, T_BANK, PICK_BANK, AUX_BANK = 0, 4, 5, 6, 7

        def bank(b, n=BANK, parts=P):
            return ps[0:parts, b * BANK:b * BANK + n]

        rows = sb("rows", [P, NJ, D])
        h_T = sb("h_T", [P, N])
        out_T = sb("out_T", [P, COLS])
        wrel = sb("wrel", [P, R, D])
        roots = sb("roots", [P, 2, D])
        biases = sb("biases", [P, 2])
        ring = sb("ring", [P, RING, G, D])
        SN = G * R * WIN
        work = sb("work", [P, 2 * SN])
        onehot_w = work[:, 0:SN].rearrange("p (t r n) -> p t r n", t=G, r=R)
        z_sb = work[:, SN:2 * SN].rearrange("p (r t n) -> p r t n", t=G, r=R)
        CW = CH * P

        def list_rows(i):
            return work[:, i * CW:(i + 1) * CW].rearrange("p (c e) -> p c e", e=P)

        dst_i, src_i, rel_i = (list_rows(i).bitcast(I32) for i in range(3))
        dst_f, src_f, rel_f = (list_rows(i) for i in range(3))
        dl_f = list_rows(3)
        NQ = NT // QUAD
        QMAXR = -(-N // QWIN)
        at = 4 * CW

        def row(n):
            nonlocal at
            at += n
            assert at <= 2 * SN
            return work[0:1, at - n:at]

        max_f, delta, round_no, round_on_q, qmax = row(NT), row(NT), row(MAXR), row(QMAXR), row(NQ)
        assert MAXR <= CW
        round_on = work[0:1, 0:MAXR]
        src_tab = sb("src_tab", [P, NT])
        rel_tab = sb("rel_tab", [P, NT])
        dl_tab = sb("dl_tab", [P, NT])
        dlq_tab = sb("dlq_tab", [P, NT])
        w_tab = sb("w_tab", [P, NT])
        inv = sb("inv", [RELP, QCOLS])
        hot_rel = sb("hot_rel", [P, 2, G, RELP], BF16)
        hot_node = sb("hot_node", [P, 2, G, WIN], BF16)
        hot_quad = sb("hot_quad", [P, 2, G, QWIN], BF16)
        rel_T = sb("rel_T", [RELP, G, P])
        node_w = sb("node_w", [P, G, WIN])
        w_part = sb("w_part", [P, G])
        staged = sb("staged", [P, RING, G], I32)
        ident = sb("ident", [P, P])
        ident_b = sb("ident_b", [P, P], BF16)
        ones = sb("ones", [P, P])
        iota0 = sb("iota0", [P, QWIN])
        iota_node = sb("iota_node", [P, WIN])
        iota_quad = sb("iota_quad", [P, QWIN])
        dmin = sb("dmin", [P, CH])
        dmax = sb("dmax", [P, CH])
        base_f = sb("base_f", [1, NT])
        win_at = sb("win_at", [1, 1])
        base_i = sb("base_i", [1, NT], I32)
        qmin = sb("qmin", [1, NQ])
        qbase_i = sb("qbase_i", [1, NQ], I32)
        spans = sb("spans", [1, 2])
        nrounds_f = sb("nrounds_f", [1, 2])
        nrounds_i = sb("nrounds_i", [1, 2], I32)
        stats = sb("stats", [P, NJ, 6])
        meanvar = sb("meanvar", [P, NJ, 2])
        std = sb("std", [P, NJ])
        rstd = sb("rstd", [P, NJ])
        shift = sb("shift", [P, NJ])

        pads_set = sem("pads_set")
        dst_in, src_in, rel_in = sem("dst_in"), sem("src_in"), sem("rel_in")
        x_in = [sem(f"x_in{c}") for c in range(NLN)]
        w_in, small_in = sem("w_in"), sem("small_in")
        consts = sem("consts")
        ident_ready = sem("ident_ready")
        lists_f = sem("lists_f")
        dl_ready = sem("dl_ready")
        prep = sem("prep")
        turned = sem("turned")
        tabs = sem("tabs")
        base_out = sem("base_out")
        delta_ready = sem("delta_ready")
        delta_spread = sem("delta_spread")
        rounds_ready = sem("rounds_ready")
        ln_var = sem("ln_var")
        ln_std = sem("ln_std")
        ln_chain = sem("ln_chain")
        ln_scale = sem("ln_scale")
        ln_done = sem("ln_done")
        h_stored = sem("h_stored")
        q_hot = sem("q_hot")
        q_counted = sem("q_counted")
        q_added = sem("q_added")
        q_base = sem("q_base")
        q_next = sem("q_next")
        inv_chain = sem("inv_chain")
        inv_made = sem("inv_made")
        hT_turned = sem("hT_turned")
        hT_made = sem("hT_made")
        root_made = sem("root_made")
        root_out = sem("root_out")
        tail_zero = sem("tail_zero")

        def layer_sems(n):
            names = ("idx_staged begun base_ready base_next hot_made t_made t_evac pick_made node_w_made w_sum w_added "
                     "s_made z_made z_evac rel_made added").split()
            d = {name: sem(f"{name}_{n}") for name in names}
            d["gathered"] = [sem(f"gathered{u}_{n}") for u in range(RING)]
            return d

        L1, L2 = layer_sems(1), layer_sems(2)
        w2_in = sem("w2_in")
        h1_turned, h1_act, h1_dve = sem("h1_turned"), sem("h1_act"), sem("h1_dve")
        h1_stored = sem("h1_stored")
        h1T_made = sem("h1T_made")
        root2_made, root2_out = sem("root2_made"), sem("root2_out")
        x_again = sem("x_again")
        y_turned, y_made, y_stored = sem("y_turned"), sem("y_made"), sem("y_stored")

        def node_cols(a, j0, nj):
            return a[:, 0:N].rearrange("h (p j) -> h j p", j=NJ)[:, j0:j0 + nj, :]

        block = ctx.enter_context(nc.Block())

        @block.sync
        def _(sp):
            whole = (CH - 1) * P * P
            left = FULL - (CH - 1) * P
            sp.wait_ge(pads_set, 3)
            for a, rows_i, s in ((dst, dst_i, dst_in), (src, src_i, src_in), (rel, rel_i, rel_in)):
                sp.dma_start(rows_i[:, 0:CH - 1, :], a[0:whole].rearrange("(c p e) -> p c e", p=P, e=P)).then_inc(s, 16)
                sp.dma_start(rows_i[0:left, CH - 1, :],
                             a[whole:FULL * P].rearrange("(p e) -> p e", e=P)).then_inc(s, 16)
                sp.dma_start(rows_i[left:left + 1, CH - 1, 0:LAST],
                             a[FULL * P:E].rearrange("(o e) -> o e", o=1)).then_inc(s, 16)
            for tile, e0 in ((left, LAST), (left + 1, 0)):
                reps, rest = divmod(P - e0, LAST)
                real = dst[FULL * P:E].rearrange("(o e) -> o e", o=1)
                sp.dma_start(dst_i[tile:tile + 1, CH - 1, e0:e0 + reps * LAST].rearrange("o (r e) -> o r e", e=LAST),
                             real.unsqueeze(1).to_broadcast([1, reps, LAST])).then_inc(dst_in, 16)
                sp.dma_start(dst_i[tile:tile + 1, CH - 1, e0 + reps * LAST:P], real[:, 0:rest]).then_inc(dst_in, 16)
            sp.dma_start(roots[:, 0, :], root1).then_inc(small_in, 16)
            sp.dma_start(roots[:, 1, :], root2).then_inc(small_in, 16)
            sp.dma_start(biases[:, 0:1], b1.rearrange("(h o) -> h o", o=1)).then_inc(small_in, 16)
            sp.dma_start(biases[:, 1:2], b2.rearrange("(h o) -> h o", o=1)).then_inc(small_in, 16)
            for r in range(R):
                sp.dma_start(wrel[:, r, :], w1[r]).then_inc(w_in, 16)
            for c in range(NLN):
                sp.wait_ge(ln_done, c + 1)
                sp.dma_start(rows_of(table1)[:, c * LNC:(c + 1) * LNC, :],
                             rows[0:NP, c * LNC:(c + 1) * LNC, :]).then_inc(h_stored, 16)
            for q in range(JQ):
                nj = min(4, NJ - 4 * q)
                sp.wait_ge(h1_dve if q % 2 else h1_act, q // 2 + 1)
                sp.dma_start(rows_of(table2)[:, 4 * q:4 * q + nj, :],
                             rows[0:NP, 4 * q:4 * q + nj, :]).then_inc(h1_stored, 16)
            sp.wait_ge(h1_turned, 1)
            for r in range(R):
                sp.dma_start(wrel[:, r, :], w2[r]).then_inc(w2_in, 16)
            sp.wait_ge(h1_stored, 16 * JQ)
            sp.dma_start(rows[0:NP, :, :], rows_of(x)).then_inc(x_again, 16)
            for q in range(JQ):
                nj = min(4, NJ - 4 * q)
                sp.wait_ge(y_made, q + 1)
                sp.dma_start(rows_of(out)[:, 4 * q:4 * q + nj, :],
                             rows[0:NP, 4 * q:4 * q + nj, :]).then_inc(y_stored, 16)
            sp.wait_ge(y_stored, 16 * JQ)

        @block.gpsimd
        def _(pool):
            nc.gpsimd.memset(ident[:], 0.0).then_inc(consts, 1)
            nc.gpsimd.memset(ones[:], 1.0).then_inc(consts, 1)
            nc.gpsimd.iota(iota0[:], [[1, QWIN]], 0, 0, allow_small_or_imprecise_dtypes=True).then_inc(consts, 1)
            nc.gpsimd.iota(round_no, [[1, MAXR]], 0, 0, allow_small_or_imprecise_dtypes=True).then_inc(consts, 1)
            pool.wait_ge(consts, 4)
            nc.gpsimd.affine_select(out=ident[:], in_=ident[:], compare_op=ALU.not_equal, fill=1.0, base=0,
                                    pattern=[[-1, P]], channel_multiplier=1).then_inc(ident_ready, 1)
            pool.wait_ge(ident_ready, 1)
            nc.gpsimd.tensor_copy(ident_b[:], ident[:]).then_inc(ident_ready, 1)
            pool.wait_ge(rounds_ready, 1)
            rounds = pool.value_load(nrounds_i[0:1, 0:1], min_val=1, max_val=MAXR)

            def gathers(L, table, stored, n_stored):
                pool.wait_ge(stored, n_stored)
                with pool.Fori(0, rounds) as k:
                    with pool.Fori(0, NI) as i:
                        for u in range(RING):
                            pool.wait_ge(L["idx_staged"], k * NG + i * RING + (u + 1))
                            pool.sem_inc(L["begun"], 1)
                            for t in range(G):
                                nc.gpsimd.indirect_dma_start(
                                    ring[:, u, t, :], None, table,
                                    bass.IndirectOffsetOnAxis(ap=staged[:, u, t:t + 1], axis=0),
                                ).then_inc(L["gathered"][u], 16)

            gathers(L1, table1, h_stored, 16 * NLN)
            gathers(L2, table2, h1_stored, 16 * JQ)

        @block.scalar
        def _(act):
            for L in (L1, L2):
                act.sem_inc(L["z_evac"], Z_BANKS)
            act.sem_inc(L1["t_evac"], SEED)
            for c in range(NLN):
                act.dma_start(rows[0:NP, c * LNC:(c + 1) * LNC, :],
                              rows_of(x)[:, c * LNC:(c + 1) * LNC, :]).then_inc(x_in[c], 16)
            act.wait_ge(src_in, 48)
            nc.scalar.copy(src_f, src_i).then_inc(lists_f, 1)
            act.wait_ge(rel_in, 48)
            nc.scalar.copy(rel_f, rel_i).then_inc(lists_f, 1)
            act.wait_ge(turned, 2)
            nc.scalar.copy(src_tab[:], bank(0, NT)).then_inc(tabs, 1)
            nc.scalar.copy(rel_tab[:], bank(2, NT)).then_inc(tabs, 1)

            def stage(L, u, col):
                act.wait_ge(tabs, 2)
                nc.scalar.copy(staged[:, u, :], src_tab[:, ds(col, G)]).then_inc(L["idx_staged"], 1)

            for u in range(RING):
                stage(L1, u, u * G)
            for c in range(NLN):
                j = slice(c * LNC, (c + 1) * LNC)
                act.wait_ge(ln_var, c + 1)
                nc.scalar.activation(std[0:NP, j], std[0:NP, j], ACT.Sqrt).then_inc(ln_std, 1)
                act.wait_ge(ln_scale, c + 1)
                for jj in range(c * LNC, (c + 1) * LNC):
                    last = nc.scalar.activation(rows[0:NP, jj, :], rows[0:NP, jj, :], ACT.Relu,
                                                bias=shift[0:NP, jj:jj + 1], scale=rstd[0:NP, jj:jj + 1])
                last.then_inc(ln_done, 1)
            for q in range(JQ):
                nj = min(4, NJ - 4 * q)
                act.wait_ge(hT_turned, q + 1)
                nc.scalar.copy(node_cols(h_T, 4 * q, nj),
                               bank(6 + q % 2, nj * NP).rearrange("h (j p) -> h j p", p=NP)).then_inc(hT_made, 1)

            def root_to_out(layer, made, went):
                for c in range(NCH):
                    n = min(BANK, N - c * BANK)
                    act.wait_ge(made, c + 1)
                    nc.scalar.activation(out_T[:, c * BANK:c * BANK + n], bank(c % 4, n), ACT.Identity,
                                         bias=biases[:, layer:layer + 1]).then_inc(went, 1)

            act.wait_ge(small_in, 64)
            root_to_out(0, root_made, root_out)
            act.wait_ge(rounds_ready, 1)
            rounds = act.value_load(nrounds_i[0:1, 0:1], min_val=1, max_val=MAXR)

            def spread_rel(L, p):
                act.wait_ge(L["pick_made"], p * QG + SEED)
                for c in range(QG):
                    act.wait_ge(L["t_made"], p * QG + (c + 1))
                    nc.scalar.copy(rel_T[:, c * QUAD:(c + 1) * QUAD, :].rearrange("r t e -> r (t e)"),
                                   bank(T_BANK, QUAD * P, RELP)).then_inc(L["t_evac"], 1)

            def layer(L, first):
                with act.Fori(0, rounds) as k:
                    if not first:
                        pass
                    if first:
                        spread_rel(L, k * NG)
                        spread_rel(L, k * NG + 1)

                    def body(i, last):
                        for u in range(RING):
                            g = k * NG + i * RING + u
                            for j in range(G // 2):
                                act.wait_ge(L["z_made"], g * (G // 2) + (j + 1))
                                nc.scalar.copy(
                                    z_sb[:, :, 2 * j:2 * j + 2, :].rearrange("h r t n -> h t r n"),
                                    bank(Z_BANK + j % Z_BANKS, 2 * R * WIN).rearrange("h (t r n) -> h t r n", t=2, r=R),
                                ).then_inc(L["z_evac"], 1)
                            if first and not (last and u >= RING - 2):
                                spread_rel(L, g + 2)
                            stage(L, u, u * G if last else (i + 1) * (RING * G) + u * G)

                    with act.Fori(0, NI - 1) as i:
                        body(i, False)
                    body(NI - 1, True)

            layer(L1, True)
            for q in range(0, JQ, 2):
                nj = min(4, NJ - 4 * q)
                act.wait_ge(h1_turned, q + 1)
                nc.scalar.activation(rows[0:NP, 4 * q:4 * q + nj, :].rearrange("p j d -> p (j d)"),
                                     bank(q % 4, nj * D, NP), ACT.Relu).then_inc(h1_act, 1)
            for u in range(RING):
                stage(L2, u, u * G)
            root_to_out(1, root2_made, root2_out)
            layer(L2, False)

        @block.vector
        def _(dve):
            for s in (q_added, *(L[n] for L in (L1, L2) for n in ("node_w_made", "added", "s_made"))):
                dve.sem_inc(s, SEED)
            nc.vector.memset(dst_i[:, CH - 1, :], 0).then_inc(pads_set, 1)
            nc.vector.memset(src_i[:, CH - 1, :], 0).then_inc(pads_set, 1)
            nc.vector.memset(rel_i[:, CH - 1, :], -1).then_inc(pads_set, 1)
            nc.vector.memset(inv[:], 0.0).then_inc(tail_zero, 1)
            nc.vector.memset(w_tab[:], 0.0).then_inc(tail_zero, 1)
            nc.vector.memset(out_T[:, N:COLS], 0.0).then_inc(tail_zero, 1)
            dve.wait_ge(dst_in, 112)
            nc.vector.tensor_copy(dst_f, dst_i).then_inc(prep, 1)
            dve.wait_ge(prep, 1)
            nc.vector.tensor_reduce(dmin[:], dst_f, AX.X, ALU.min).then_inc(prep, 1)
            nc.vector.tensor_reduce(dmax[:], dst_f, AX.X, ALU.max).then_inc(prep, 1)
            dve.wait_ge(prep, 2)
            nc.vector.tensor_tensor(dl_f, dst_f, dmin[:].unsqueeze(2).to_broadcast([P, CH, P]),
                                    ALU.subtract).then_inc(dl_ready, 1)
            for c in range(NLN):
                js = range(c * LNC, (c + 1) * LNC)
                j = slice(c * LNC, (c + 1) * LNC)
                dve.wait_ge(x_in[c], 16)
                for jj in js:
                    last = nc.vector.bn_stats(stats[0:NP, jj, :], rows[0:NP, jj, :])
                last.then_inc(ln_chain, 1)
                dve.wait_ge(ln_chain, 3 * c + 1)
                for jj in js:
                    last = nc.vector.bn_aggr(meanvar[0:NP, jj, :], stats[0:NP, jj, :])
                last.then_inc(ln_chain, 1)
                dve.wait_ge(ln_chain, 3 * c + 2)
                nc.vector.tensor_scalar(std[0:NP, j], meanvar[0:NP, j, 1], EPS, None, ALU.add).then_inc(ln_var, 1)
                dve.wait_ge(ln_std, c + 1)
                nc.vector.reciprocal(rstd[0:NP, j], std[0:NP, j]).then_inc(ln_chain, 1)
                dve.wait_ge(ln_chain, 3 * c + 3)
                nc.vector.scalar_tensor_tensor(out=shift[0:NP, j], in0=meanvar[0:NP, j, 0], scalar=-1.0,
                                               in1=rstd[0:NP, j], op0=ALU.mult, op1=ALU.mult).then_inc(ln_scale, 1)
            dve.wait_ge(turned, 4)
            nc.vector.tensor_copy(dl_tab[:], bank(4, NT)).then_inc(base_out, 1)
            nc.vector.tensor_copy(base_f[:], ps[0:1, 6 * BANK:6 * BANK + NT]).then_inc(base_out, 1)
            dve.wait_ge(turned, 5)
            nc.vector.tensor_copy(max_f, ps[0:1, 0:NT]).then_inc(base_out, 1)
            dve.wait_ge(base_out, 3)
            quads = lambda a: a.rearrange("o (q t) -> o q t", t=QUAD)
            nc.vector.tensor_reduce(qmin[:], quads(base_f[:]), AX.X, ALU.min).then_inc(base_out, 1)
            nc.vector.tensor_reduce(qmax, quads(max_f), AX.X, ALU.max).then_inc(base_out, 1)
            dve.wait_ge(base_out, 5)
            nc.vector.tensor_tensor(quads(delta), quads(base_f[:]), qmin[:].unsqueeze(2).to_broadcast([1, NQ, QUAD]),
                                    ALU.subtract).then_inc(delta_ready, 1)
            nc.vector.tensor_tensor(max_f, max_f, base_f[:], ALU.subtract).then_inc(base_out, 1)
            nc.vector.tensor_tensor(qmax, qmax, qmin[:], ALU.subtract).then_inc(base_out, 1)
            dve.wait_ge(base_out, 7)
            nc.vector.tensor_reduce(spans[:, 0:1], max_f, AX.X, ALU.max).then_inc(base_out, 1)
            nc.vector.tensor_reduce(spans[:, 1:2], qmax, AX.X, ALU.max).then_inc(base_out, 1)
            dve.wait_ge(consts, 4)
            dve.wait_ge(base_out, 9)
            nc.vector.tensor_scalar(round_on, round_no, float(WIN), spans[:, 0:1], ALU.mult,
                                    ALU.is_le).then_inc(base_out, 1)
            nc.vector.tensor_scalar(round_on_q, round_no[:, 0:QMAXR], float(QWIN), spans[:, 1:2], ALU.mult,
                                    ALU.is_le).then_inc(base_out, 1)
            dve.wait_ge(base_out, 11)
            nc.vector.tensor_reduce(nrounds_f[:, 0:1], round_on, AX.X, ALU.add).then_inc(base_out, 1)
            nc.vector.tensor_reduce(nrounds_f[:, 1:2], round_on_q, AX.X, ALU.add).then_inc(base_out, 1)
            dve.wait_ge(base_out, 13)
            nc.vector.tensor_copy(nrounds_i[:], nrounds_f[:]).then_inc(rounds_ready, 1)
            dve.wait_ge(delta_spread, 1)
            nc.vector.tensor_tensor(dlq_tab[:], dl_tab[:], bank(2, NT), ALU.add).then_inc(base_out, 1)
            nc.vector.tensor_copy(iota_quad[:], iota0[:]).then_inc(base_out, 1)
            nc.vector.tensor_scalar(qbase_i[:], qmin[:], float(QCOLS - QWIN), None, ALU.min).then_inc(q_base, 1)
            dve.wait_ge(base_out, 15)
            dve.wait_ge(rounds_ready, 1)
            rounds = dve.value_load(nrounds_i[0:1, 0:1], min_val=1, max_val=MAXR)
            qrounds = dve.value_load(nrounds_i[0:1, 1:2], min_val=1, max_val=MAXR)
            dve.wait_ge(tabs, 2)

            def hot_relations(b, col, width):
                return nc.vector.tensor_tensor(
                    hot_rel[:, b, :, 0:width], iota0[:, 0:width].unsqueeze(1).to_broadcast([P, G, width]),
                    rel_tab[:, ds(col, G)].unsqueeze(2).to_broadcast([P, G, width]), ALU.is_equal)

            def quad_hots(b, col):
                hot_relations(b, col, R)
                nc.vector.tensor_tensor(
                    hot_quad[:, b, :, :], iota_quad[:].unsqueeze(1).to_broadcast([P, G, QWIN]),
                    dlq_tab[:, ds(col, G)].unsqueeze(2).to_broadcast([P, G, QWIN]), ALU.is_equal).then_inc(q_hot, 1)

            with dve.Fori(0, qrounds) as k:
                dve.wait_ge(q_base, 1 + k)
                quad_hots(0, 0)

                def count_body(i, last):
                    for u in range(2):
                        g = k * NG + i * 2 + u
                        if not (last and u == 1):
                            quad_hots((u + 1) % 2, i * (2 * G) + (u + 1) * G)
                        dve.wait_ge(tail_zero, 3)
                        _, at = nc.values_load_multi_w_load_instructions(
                            qbase_i[0:1, ds(i * (2 * QG) + u * QG, QG)], engines=[mybir.EngineType.DVE],
                            min_val=0, max_val=QCOLS - QWIN,
                            skip_runtime_bounds_check_because="the row was clamped to its bounds when it was written")
                        dve.wait_ge(q_counted, g + 1)
                        for c in range(QG):
                            dve.wait_ge(q_added, g * QG + (c + SEED))
                            nc.vector.tensor_tensor(
                                inv[0:R, ds(at[c], QWIN)], inv[0:R, ds(at[c], QWIN)],
                                ps[0:R, (4 + u) * BANK + c * QWIN:(4 + u) * BANK + (c + 1) * QWIN],
                                ALU.add).then_inc(q_added, 1)

                with dve.Fori(0, NG // 2 - 1) as i:
                    count_body(i, False)
                count_body(NG // 2 - 1, True)
                nc.vector.tensor_scalar(iota_quad[:], iota_quad[:], float(QWIN), None, ALU.add).then_inc(q_next, 1)
                nc.vector.tensor_scalar(qmin[:], qmin[:], float(QWIN), None, ALU.add).then_inc(q_next, 1)
                dve.wait_ge(q_next, k * 2 + 2)
                nc.vector.tensor_scalar(qbase_i[:], qmin[:], float(QCOLS - QWIN), None, ALU.min).then_inc(q_base, 1)
            dve.wait_ge(q_added, qrounds * (NG * QG) + SEED)
            nc.vector.tensor_scalar(inv[:], inv[:], 1.0, None, ALU.max).then_inc(inv_chain, 1)
            dve.wait_ge(inv_chain, 1)
            nc.vector.reciprocal(inv[:], inv[:]).then_inc(inv_made, 1)

            def layer(L, first):
                nc.vector.tensor_copy(iota_node[:], iota0[:, 0:WIN]).then_inc(L["base_next"], 1)
                nc.vector.memset(win_at[:], 0.0).then_inc(L["base_next"], 1)
                dve.wait_ge(L["base_next"], 2)
                nc.vector.tensor_scalar(base_i[:], base_f[:], win_at[:], float(COLS - WIN), ALU.add, ALU.min)\
                    .then_inc(L["base_ready"], 1)

                def hots(b, col):
                    nc.vector.tensor_tensor(
                        hot_node[:, b, :, :], iota_node[:].unsqueeze(1).to_broadcast([P, G, WIN]),
                        dl_tab[:, ds(col, G)].unsqueeze(2).to_broadcast([P, G, WIN]), ALU.is_equal)
                    hot_relations(b, col, RELP).then_inc(L["hot_made"], 1)

                def weighted(p, b, col, before):
                    if first:
                        dve.wait_ge(L["pick_made"], p * QG + (QG + SEED))
                        w_by_node = bank(PICK_BANK, G * WIN).rearrange("p (t n) -> p t n", n=WIN)
                    else:
                        dve.wait_ge(L["hot_made"], p + 1)
                        w_by_node = w_tab[:, ds(col, G)].unsqueeze(2).to_broadcast([P, G, WIN])
                    nc.vector.tensor_tensor(node_w[:], hot_node[:, b, :, :], w_by_node, ALU.mult)\
                        .then_inc(L["node_w_made"], 1)
                    dve.wait_ge(L["node_w_made"], p + (1 + SEED))
                    for h in range(2):
                        if before is not None:
                            dve.wait_ge(L["z_made"], before * (G // 2) + (h + 1) * (G // 4))
                        t = slice(h * G // 2, (h + 1) * G // 2)
                        nc.vector.tensor_tensor(
                            onehot_w[:, t, :, :],
                            hot_rel[:, b, t, 0:R].unsqueeze(3).to_broadcast([P, G // 2, R, WIN]),
                            node_w[:, t, :].unsqueeze(2).to_broadcast([P, G // 2, R, WIN]),
                            ALU.mult).then_inc(L["s_made"], 1)
                    if first:
                        nc.vector.tensor_reduce(w_part[:], node_w[:], AX.X, ALU.add).then_inc(L["w_sum"], 1)
                        dve.wait_ge(L["w_sum"], p + 1)
                        nc.vector.tensor_tensor(w_tab[:, ds(col, G)], w_tab[:, ds(col, G)], w_part[:],
                                                ALU.add).then_inc(L["w_added"], 1)

                with dve.Fori(0, rounds) as k:
                    dve.wait_ge(L["base_ready"], k + 1)
                    dve.wait_ge(L["s_made"], k * (2 * NG) + SEED)
                    hots(0, 0)
                    hots(1, G)
                    weighted(k * NG, 0, 0, None)

                    def body(i, last):
                        for u in range(RING):
                            g = k * NG + i * RING + u
                            col = i * (RING * G) + u * G
                            if not (last and u >= RING - 2):
                                dve.wait_ge(L["s_made"], g * 2 + (2 + SEED))
                                hots(u % 2, col + 2 * G)
                            if not (last and u == RING - 1):
                                weighted(g + 1, (u + 1) % 2, col + G, g)
                            dve.wait_ge(tail_zero, 3)
                            _, at = nc.values_load_multi_w_load_instructions(
                                base_i[0:1, ds(col, G)], engines=[mybir.EngineType.DVE],
                                min_val=0, max_val=COLS - WIN,
                                skip_runtime_bounds_check_because="the row was clamped to its bounds when written")
                            dve.wait_ge(L["rel_made"], g + 1)
                            for t in range(G):
                                dve.wait_ge(L["added"], g * G + (t + SEED))
                                nc.vector.tensor_tensor(
                                    out_T[:, ds(at[t], WIN)], out_T[:, ds(at[t], WIN)],
                                    ps[:, REL_BANK * BANK + t * WIN:REL_BANK * BANK + (t + 1) * WIN],
                                    ALU.add).then_inc(L["added"], 1)

                    with dve.Fori(0, NI - 1) as i:
                        body(i, False)
                    body(NI - 1, True)
                    nc.vector.tensor_scalar(iota_node[:], iota_node[:], float(WIN), None, ALU.add)\
                        .then_inc(L["base_next"], 1)
                    nc.vector.tensor_scalar(win_at[:], win_at[:], float(WIN), None, ALU.add)\
                        .then_inc(L["base_next"], 1)
                    dve.wait_ge(L["base_next"], k * 2 + 4)
                    nc.vector.tensor_scalar(base_i[:], base_f[:], win_at[:], float(COLS - WIN), ALU.add, ALU.min)\
                        .then_inc(L["base_ready"], 1)

            dve.wait_ge(root_out, NCH)
            layer(L1, True)
            for q in range(1, JQ, 2):
                nj = min(4, NJ - 4 * q)
                dve.wait_ge(h1_turned, q + 1)
                nc.vector.tensor_scalar(rows[0:NP, 4 * q:4 * q + nj, :].rearrange("p j d -> p (j d)"),
                                        bank(q % 4, nj * D, NP), 0.0, None, ALU.max).then_inc(h1_dve, 1)
            dve.wait_ge(L1["added"], rounds * (NG * G) + SEED)
            nc.vector.tensor_scalar(h_T[:], out_T[:, 0:N], 0.0, None, ALU.max).then_inc(h1T_made, 1)
            dve.wait_ge(root2_out, NCH)
            layer(L2, False)
            dve.wait_ge(x_again, 16)
            for q in range(JQ):
                nj = min(4, NJ - 4 * q)
                r = rows[0:NP, 4 * q:4 * q + nj, :].rearrange("p j d -> p (j d)")
                dve.wait_ge(y_turned, q + 1)
                nc.vector.tensor_tensor(r, r, bank(q % 4, nj * D, NP), ALU.add).then_inc(y_made, 1)

        @block.tensor
        def _(pe):
            pe.sem_inc(L1["pick_made"], SEED)
            pe.wait_ge(ident_ready, 2)
            for n, (a, s, need, b) in enumerate(((src_f, lists_f, 1, 0), (rel_f, lists_f, 2, 2), (dl_f, dl_ready, 1, 4))):
                pe.wait_ge(s, need)
                for c in range(CH):
                    w = min(P, NT - c * P)
                    last = nc.tensor.transpose(ps[:, b * BANK + c * P:b * BANK + c * P + w], a[0:w, c, :],
                                               ident[0:w, 0:w])
                last.then_inc(turned, 1)

            def row_of(col, b):
                for c in range(CH):
                    last = nc.tensor.transpose(ps[0:1, b * BANK + c * P:b * BANK + (c + 1) * P], col[:, c:c + 1],
                                               ident[:])
                last.then_inc(turned, 1)

            row_of(dmin, 6)
            pe.wait_ge(prep, 3)
            pe.wait_ge(tabs, 1)
            row_of(dmax, 0)
            pe.wait_ge(consts, 4)
            pe.wait_ge(tabs, 2)
            pe.wait_ge(delta_ready, 1)
            for c in range(0, NT, BANK):
                n = min(BANK, NT - c)
                last = nc.tensor.matmul(bank(2 + c // BANK, n), ones[0:1, :], delta[:, c:c + n], start=True, stop=True)
            last.then_inc(delta_spread, 1)
            pe.wait_ge(rounds_ready, 1)
            rounds = pe.value_load(nrounds_i[0:1, 0:1], min_val=1, max_val=MAXR)
            qrounds = pe.value_load(nrounds_i[0:1, 1:2], min_val=1, max_val=MAXR)
            pe.wait_ge(base_out, 3)

            with pe.Fori(0, qrounds) as k:
                with pe.Fori(0, NG // 2) as i:
                    for u in range(2):
                        g = k * NG + i * 2 + u
                        pe.wait_ge(q_hot, g + 1)
                        for t in range(G):
                            c = t // QUAD
                            last = nc.tensor.matmul(
                                ps[0:R, (4 + u) * BANK + c * QWIN:(4 + u) * BANK + (c + 1) * QWIN],
                                hot_rel[:, u, t, 0:R], hot_quad[:, u, t, :], start=t % QUAD == 0,
                                stop=t % QUAD == QUAD - 1)
                        last.then_inc(q_counted, 1)

            pe.wait_ge(ln_done, NLN)
            for q in range(JQ):
                nj = min(4, NJ - 4 * q)
                if q >= 2:
                    pe.wait_ge(hT_made, q - 1)
                for j in range(nj):
                    last = nc.tensor.transpose(bank(6 + q % 2, 4 * NP)[:, j * NP:(j + 1) * NP],
                                               rows[0:NP, 4 * q + j, :], ident[0:NP, 0:NP])
                last.then_inc(hT_turned, 1)

            def root_products(layer, made, went, table_ready, n):
                pe.wait_ge(table_ready, n)
                for c in range(NCH):
                    n = min(BANK, N - c * BANK)
                    if c >= 4:
                        pe.wait_ge(went, c - 3)
                    nc.tensor.matmul(bank(c % 4, n), roots[:, layer, :], h_T[:, c * BANK:c * BANK + n], start=True,
                                     stop=True).then_inc(made, 1)

            pe.wait_ge(small_in, 64)
            root_products(0, root_made, root_out, hT_made, JQ)
            pe.wait_ge(w_in, 16 * R)
            pe.wait_ge(root_out, NCH)

            def rel_turn(L, p, c, b):
                if c == 0:
                    pe.wait_ge(L["hot_made"], p + 1)
                pe.wait_ge(L["t_evac"], p * QG + (c + SEED))
                for t in range(QUAD):
                    last = nc.tensor.matmul(ps[0:RELP, T_BANK * BANK + t * P:T_BANK * BANK + (t + 1) * P],
                                            hot_rel[:, b, c * QUAD + t, :], ident_b[:], start=True, stop=True)
                last.then_inc(L["t_made"], 1)

            def pick(L, p, c, at):
                if c == 0:
                    pe.wait_ge(L["node_w_made"], p + SEED)
                pe.wait_ge(L["t_evac"], p * QG + (c + 1 + SEED))
                pe.wait_ge(inv_made, 1)
                for t in range(c * QUAD, (c + 1) * QUAD):
                    last = nc.tensor.matmul(ps[:, PICK_BANK * BANK + t * WIN:PICK_BANK * BANK + (t + 1) * WIN],
                                            rel_T[:, t, :], inv[:, ds(at[t], WIN)], start=True, stop=True)
                last.then_inc(L["pick_made"], 1)

            def windows(col):
                return nc.values_load_multi_w_load_instructions(
                    base_i[0:1, ds(col, G)], engines=[mybir.EngineType.PE], min_val=0, max_val=COLS - WIN,
                    skip_runtime_bounds_check_because="the row was clamped to its bounds when it was written")[1]

            def layer(L, first):
                with pe.Fori(0, rounds) as k:
                    if first:
                        for p in range(2):
                            for c in range(QG):
                                rel_turn(L, k * NG + p, c, p)
                                if c == 0:
                                    at = windows(p * G)
                                pick(L, k * NG + p, c, at)

                    def body(i, last):
                        for u in range(RING):
                            g = k * NG + i * RING + u
                            ahead = first and not (last and u >= RING - 2)
                            if ahead:
                                at = windows(i * (RING * G) + (u + 2) * G)
                            pe.wait_ge(L["gathered"][u], (k * NI + i) * (16 * G) + 16 * G)
                            for j in range(G // 2):
                                if j % (G // 4) == 0:
                                    pe.wait_ge(L["s_made"], g * 2 + (j // (G // 4) + 1 + SEED))
                                pe.wait_ge(L["z_evac"], g * (G // 2) + (j + 1))
                                for t in (2 * j, 2 * j + 1):
                                    mm = nc.tensor.matmul(
                                        bank(Z_BANK + j % Z_BANKS, 2 * R * WIN)[:, t % 2 * R * WIN:(t % 2 + 1) * R * WIN],
                                        ring[:, u, t, :], onehot_w[:, t, :, :].rearrange("p r n -> p (r n)"),
                                        start=True, stop=True)
                                mm.then_inc(L["z_made"], 1)
                            if ahead:
                                rel_turn(L, g + 2, 0, u % 2)
                            pe.wait_ge(L["z_evac"], g * (G // 2) + (G // 2 + Z_BANKS))
                            pe.wait_ge(L["added"], g * G + SEED)
                            for r in range(R):
                                mm = nc.tensor.matmul(bank(REL_BANK, G * WIN), wrel[:, r, :],
                                                      z_sb[:, r, :, :].rearrange("h t n -> h (t n)"),
                                                      start=(r == 0), stop=(r == R - 1))
                                if ahead and r % QUAD == QUAD - 1:
                                    c = r // QUAD
                                    pick(L, g + 2, c, at)
                                    if c < QG - 1:
                                        rel_turn(L, g + 2, c + 1, u % 2)
                            mm.then_inc(L["rel_made"], 1)

                    with pe.Fori(0, NI - 1) as i:
                        body(i, False)
                    body(NI - 1, True)

            def out_rows(L, turned_s, ready):
                pe.wait_ge(L["added"], rounds * (NG * G) + SEED)
                for q in range(JQ):
                    nj = min(4, NJ - 4 * q)
                    if q >= 4:
                        ready(q)
                    for j in range(nj):
                        mm = nc.tensor.transpose(bank(q % 4, BANK, NP)[:, j * D:(j + 1) * D],
                                                 node_cols(out_T, 4 * q + j, 1).rearrange("h j p -> h (j p)"),
                                                 ident[:])
                    mm.then_inc(turned_s, 1)

            layer(L1, True)
            out_rows(L1, h1_turned, lambda q: pe.wait_ge(h1_dve if q % 2 else h1_act, (q - 4) // 2 + 1))
            pe.wait_ge(h1_act, (JQ + 1) // 2)
            pe.wait_ge(h1_dve, JQ // 2)
            root_products(1, root2_made, root2_out, h1T_made, 1)
            pe.wait_ge(w2_in, 16 * R)
            pe.wait_ge(root2_out, NCH)
            layer(L2, False)
            out_rows(L2, y_turned, lambda q: pe.wait_ge(y_made, q - 3))


_INS = ["x", "src", "dst", "edge_type_16", "L0_gnn_W1", "L0_gnn_root1", "L0_gnn_b1", "L0_gnn_W2", "L0_gnn_root2",
        "L0_gnn_b2"]


def kernel(**inputs):
    import numpy as _np
    import concourse.bacc as _bacc
    from concourse import mybir as _mybir
    from concourse.bass_utils import run_bass_kernel_spmd as _run

    nc = _bacc.Bacc("TRN2", target_bir_lowering=False, num_devices=1)
    arrays, args = {}, []
    for name in _INS:
        a = _np.ascontiguousarray(inputs[name])
        arrays[f"in_{name}_dram"] = a
        args.append(nc.dram_tensor(f"in_{name}_dram", a.shape, _mybir.dt.from_np(a.dtype), kind="ExternalInput").ap())
    shape = inputs["x"].shape
    args.append(nc.dram_tensor("out_0_dram", shape, _mybir.dt.float32, kind="ExternalOutput").ap())
    rgcn_kernel(nc, *args)
    r = _run(nc, [arrays], core_ids=[0])
    return r.results[0]["out_0_dram"]
```

```python
from contextlib import ExitStack

import concourse.bass as bass
from concourse import mybir

F32 = mybir.dt.float32
BF16 = mybir.dt.bfloat16
I32 = mybir.dt.int32
ALU = mybir.AluOpType
ACT = mybir.ActivationFunctionType
AX = mybir.AxisListType
ds = bass.ds

P = 128
EPS = 1e-5
G = 16
RING = 4
WIN = 12
QUAD = 4
QWIN = 48
QB = 4
Z_BANKS = 4
SEED = 1
SEED_C = 2
T_AT = 6
PICKS_AT = (3, 8, 13)
RELP = 32
BANK = 512


def rgcn_kernel(nc, x, src, dst, rel, w1, root1, b1, w2, root2, b2, out):
    N, D = x.shape
    E = src.shape[0]
    R = w1.shape[0]
    NT = -(-E // (P * G * RING)) * G * RING
    NG = NT // G
    NI = NG // RING
    REAL = -(-E // P) - (NG - 1) * G
    CH = -(-NT // P)
    FULL = E // P
    LAST = E - FULL * P
    NP = next(p for p in range(P, 0, -1) if N % p == 0)
    NJ = N // NP
    MAXR = -(-N // WIN)
    COLS = N + WIN + (-(N + WIN)) % 4
    QCOLS = N + QWIN + (-(N + QWIN)) % 4
    QG = G // QUAD
    assert QG * RELP == P and (QG - 1) * QUAD < REAL < G
    last_quads = [range(c * QUAD, min((c + 1) * QUAD, REAL)) for c in range(QG)]
    assert D == P and R <= RELP and FULL // P == CH - 1 and 0 < LAST < P and NT - FULL == 2
    LNC = 10
    LNP = 3
    NLN = NJ // LNC
    assert NJ % LNC == 0
    JQ = -(-NJ // 4)
    NCH = -(-N // BANK)
    assert NCH == NI and QB == RING and NJ >= G * (RING - 1)

    table1 = nc.dram_tensor("h_rows_dram", (N, D), F32).ap()
    table2 = nc.dram_tensor("h1_rows_dram", (N, D), F32).ap()
    rows_of = lambda a: a.rearrange("(p j) d -> p j d", j=NJ)

    with ExitStack() as ctx:
        def sb(name, shape, dt=F32):
            return ctx.enter_context(nc.sbuf_tensor(name, shape, dt))

        def sem(name):
            return ctx.enter_context(nc.semaphore(name))

        ps = ctx.enter_context(nc.psum_tensor("ps", [P, 8 * BANK], F32))
        Z_BANK, REL_BANK, T_BANK, PICK_BANK, AUX_BANK = 0, 4, 5, 6, 7

        def bank(b, n=BANK, parts=P):
            return ps[0:parts, b * BANK:b * BANK + n]

        rows = sb("rows", [P, NJ, D])
        h_T = sb("h_T", [P, N])
        out_T = sb("out_T", [P, COLS])
        wrel = sb("wrel", [P, R, D])
        roots = sb("roots", [P, 2, D])
        biases = sb("biases", [P, 2])
        ring = sb("ring", [P, RING, G, D])
        more_slots = [rows.rearrange("p j d -> p (j d)")[:, u * G * D:(u + 1) * G * D] for u in range(RING - 1)]\
            + [h_T[:, 0:G * D]]
        slots_2 = [ring[:, u] for u in range(RING)]
        slots_1 = slots_2 + [a.rearrange("p (t d) -> p t d", t=G) for a in more_slots]
        assert (NG % len(slots_1)) % 2 == 0 and NG % len(slots_2) == 0
        SN = G * R * WIN
        work = sb("work", [P, 2 * SN])
        onehot_w = work[:, 0:SN].rearrange("p (t r n) -> p t r n", t=G, r=R)
        z_sb = work[:, SN:2 * SN].rearrange("p (r t n) -> p r t n", t=G, r=R)
        CW = CH * P

        def list_rows(i):
            return work[:, i * CW:(i + 1) * CW].rearrange("p (c e) -> p c e", e=P)

        dst_i, src_i, rel_i = (list_rows(i).bitcast(I32) for i in range(3))
        dst_f, src_f, rel_f = (list_rows(i) for i in range(3))
        dl_f = list_rows(3)
        NQ = NT // QUAD
        QMAXR = -(-N // QWIN)
        at = 4 * CW

        def row(n):
            nonlocal at
            at += n
            assert at <= 2 * SN
            return work[0:1, at - n:at]

        delta, round_no, round_on_q, qmax = row(NT), row(MAXR), row(QMAXR), row(NQ)
        assert MAXR <= CW
        round_on = work[0:1, 0:MAXR]
        src_tab = sb("src_tab", [P, NT])
        dl_tab = sb("dl_tab", [P, NT])
        dlq_tab = sb("dlq_tab", [P, NT])
        count_tab = dlq_tab
        w_tab = sb("w_tab", [P, NT])
        rel_b = sb("rel_b", [P, NT], BF16)
        dl_b = sb("dl_b", [P, NT], BF16)
        dlq_b = sb("dlq_b", [P, NT], BF16)
        counts = sb("counts", [P, QCOLS])
        hot_rel = sb("hot_rel", [P, 2, RELP, G], BF16)
        hot_node = sb("hot_node", [P, 2, WIN, G], BF16)
        hot_rel_4 = sb("hot_rel_4", [P, QG, RELP, G], BF16)
        assert NG * QUAD * P < 1 << 16
        halves = counts[:].bitcast(BF16)
        count_lo, count_hi = (halves.rearrange("p (n s) -> p n s", s=2)[:, :, i] for i in range(2))
        rel_T = sb("rel_T", [P, G, P], BF16)
        count_hots = work[:, 0:QB * (QWIN + R) * G // 2].bitcast(BF16)
        hot_quad = count_hots[:, 0:QB * QWIN * G].rearrange("p (b n t) -> p b n t", b=QB, t=G)
        hot_quad_rel = count_hots[:, QB * QWIN * G:].rearrange("p (b n t) -> p b n t", b=QB, t=G)
        q_rows = work[0:1, QB * (QWIN + R) * G // 2:3 * CW]
        assert q_rows.shape[1] >= 2 * NQ
        qmin = q_rows[:, 0:NQ]
        qbase_i = q_rows[:, NQ:2 * NQ].bitcast(I32)
        node_c = sb("node_c", [P, G, WIN, 2])
        node_w = sb("node_w", [P, WIN, G])
        count_part = sb("count_part", [P, G])
        count_or_1 = sb("count_or_1", [P, G])
        staged = sb("staged", [P, 2 * RING, G], I32)
        ident = sb("ident", [P, P])
        ident_b = sb("ident_b", [P, P], BF16)
        ones = hot_node[0:1].rearrange("p b n t -> p (b n t)").bitcast(F32)[:, 0:P]
        iota_b = sb("iota_b", [P, QWIN, G], BF16)
        dmin = sb("dmin", [P, CH])
        dmax = sb("dmax", [P, CH])
        base_f = sb("base_f", [1, NT])
        tile_span = sb("tile_span", [P, CH])
        part_span = sb("part_span", [P, 1])
        win_at = sb("win_at", [P, 1])
        base_i = sb("base_i", [1, NT], I32)
        spans = sb("spans", [1, 2])
        nrounds_f = sb("nrounds_f", [1, 2])
        nrounds_i = sb("nrounds_i", [1, 2], I32)
        stats = ring[:, 0, :, :].rearrange("p t d -> p (t d)")[:, 0:6 * NJ].rearrange("p (j s) -> p j s", s=6)
        ln_cols = ring[:, 1, 0:6, :].rearrange("p t d -> p (t d)")
        meanvar = ln_cols[:, 0:2 * NJ].rearrange("p (j s) -> p j s", s=2)
        std, rstd, shift = (ln_cols[:, n * NJ:(n + 1) * NJ] for n in (2, 3, 4))

        pads_set = sem("pads_set")
        dst_in, src_in, rel_in = sem("dst_in"), sem("src_in"), sem("rel_in")
        x_in = [sem(f"x_in{c}") for c in range(NLN)]
        w_in, small_in = sem("w_in"), sem("small_in")
        consts = sem("consts")
        ident_ready = sem("ident_ready")
        lists_f = sem("lists_f")
        dl_ready = sem("dl_ready")
        prep = sem("prep")
        turned = sem("turned")
        tabs = sem("tabs")
        base_out = sem("base_out")
        delta_ready = sem("delta_ready")
        delta_spread = sem("delta_spread")
        rounds_ready = sem("rounds_ready")
        ln_var = sem("ln_var")
        ln_std = sem("ln_std")
        ln_stats, ln_aggr, ln_rstd = sem("ln_stats"), sem("ln_aggr"), sem("ln_rstd")
        ln_scale = sem("ln_scale")
        ln_act, ln_pool = sem("ln_act"), sem("ln_pool")
        ln_relu = sem("ln_relu")
        h_stored = sem("h_stored")
        root_done = sem("root_done")
        row_out = sem("row_out")
        q_hot = sem("q_hot")
        q_counted = sem("q_counted")
        q_added = sem("q_added")
        q_base = sem("q_base")
        q_next = sem("q_next")
        counts_made = sem("counts_made")
        tab_zero = sem("tab_zero")
        hT_turned = sem("hT_turned")
        hT_made = sem("hT_made")
        root_made = sem("root_made")
        root_out = sem("root_out")
        tail_zero = sem("tail_zero")

        def layer_sems(n):
            names = ("rel_first begun base_ready base_next hot_made t_made t_evac pick_made node_c_made count_sum count_added "
                     "hot_4_made count_max w_made node_w_made "
                     "s_made z_made z_evac rel_made added").split()
            d = {name: sem(f"{name}_{n}") for name in names}
            d["slots"] = slots_1 if n == 1 else slots_2
            d["idx_staged"] = [sem(f"idx_staged{u}_{n}") for u in range(len(d["slots"]))]
            d["gathered"] = [sem(f"gathered{u}_{n}") for u in range(len(d["slots"]))]
            d["last_quad"] = [sem(f"last_quad{c}_{n}") for c in range(QG)]
            return d

        L1, L2 = layer_sems(1), layer_sems(2)
        w2_in = sem("w2_in")
        h1_turned, h1_act, h1_dve = sem("h1_turned"), sem("h1_act"), sem("h1_dve")
        h1_stored = sem("h1_stored")
        h1T_made = sem("h1T_made")
        root2_made, root2_out = sem("root2_made"), sem("root2_out")
        x_again = sem("x_again")
        y_turned, y_made, y_stored = sem("y_turned"), sem("y_made"), sem("y_stored")

        def bodies(L):
            width = len(L["slots"])
            in_loop = (NG - 1) // width
            return width, in_loop, NG - in_loop * width

        def use_of_slot(L, u, k, i):
            width, in_loop, rest = bodies(L)
            return k * (in_loop + (u < rest)) + i + 1

        def fills_of_slot(L, u, k, i):
            width, in_loop, rest = bodies(L)
            return k * (in_loop + (u < rest - 1)) + i + 1

        def node_cols(a, j0, nj):
            return a[:, 0:N].rearrange("h (p j) -> h j p", j=NJ)[:, j0:j0 + nj, :]

        block = ctx.enter_context(nc.Block())

        @block.sync
        def _(sp):
            whole = (CH - 1) * P * P
            left = FULL - (CH - 1) * P
            sp.wait_ge(pads_set, 3)
            for a, rows_i, s in ((dst, dst_i, dst_in), (src, src_i, src_in), (rel, rel_i, rel_in)):
                sp.dma_start(rows_i[:, 0:CH - 1, :], a[0:whole].rearrange("(c p e) -> p c e", p=P, e=P)).then_inc(s, 16)
                sp.dma_start(rows_i[0:left, CH - 1, :],
                             a[whole:FULL * P].rearrange("(p e) -> p e", e=P)).then_inc(s, 16)
                real = a[FULL * P:E].rearrange("(o e) -> o e", o=1)
                sp.dma_start(rows_i[left:left + 1, CH - 1, 0:LAST], real).then_inc(s, 16)
                if a is dst:
                    reps, rest = divmod(P - LAST, LAST)
                    pad = dst_i[left:left + 1, CH - 1, LAST:P]
                    sp.dma_start(pad[:, 0:reps * LAST].rearrange("o (r e) -> o r e", e=LAST),
                                 real.unsqueeze(1).to_broadcast([1, reps, LAST])).then_inc(s, 16)
                    sp.dma_start(pad[:, reps * LAST:], real[:, 0:rest]).then_inc(s, 16)
                    sp.dma_start(dst_i[left + 1:left + 2, CH - 1, :],
                                 dst[E - P:E].rearrange("(o e) -> o e", o=1)).then_inc(s, 16)
            sp.dma_start(roots[:, 0, :], root1).then_inc(small_in, 16)
            sp.dma_start(roots[:, 1, :], root2).then_inc(small_in, 16)
            sp.dma_start(biases[:, 0:1], b1.rearrange("(h o) -> h o", o=1)).then_inc(small_in, 16)
            sp.dma_start(biases[:, 1:2], b2.rearrange("(h o) -> h o", o=1)).then_inc(small_in, 16)
            for r in range(R):
                sp.dma_start(wrel[:, r, :], w1[r]).then_inc(w_in, 16)
            for c in range(NLN):
                sp.wait_ge(ln_act, c + 1)
                sp.wait_ge(ln_pool, c + 1)
                sp.dma_start(rows_of(table1)[:, c * LNC:(c + 1) * LNC, :],
                             rows[0:NP, c * LNC:(c + 1) * LNC, :]).then_inc(h_stored, 16)
            for q in range(JQ):
                nj = min(4, NJ - 4 * q)
                sp.wait_ge(h1_dve if q % 2 else h1_act, q // 2 + 1)
                sp.dma_start(rows_of(table2)[:, 4 * q:4 * q + nj, :],
                             rows[0:NP, 4 * q:4 * q + nj, :]).then_inc(h1_stored, 16)
            sp.wait_ge(h1_turned, 1)
            for r in range(R):
                sp.dma_start(wrel[:, r, :], w2[r]).then_inc(w2_in, 16)
            sp.wait_ge(h1_stored, 16 * JQ)
            sp.dma_start(rows[0:NP, :, :], rows_of(x)).then_inc(x_again, 16)
            for q in range(JQ):
                nj = min(4, NJ - 4 * q)
                sp.wait_ge(y_made, q + 1)
                sp.dma_start(rows_of(out)[:, 4 * q:4 * q + nj, :],
                             rows[0:NP, 4 * q:4 * q + nj, :]).then_inc(y_stored, 16)
            sp.wait_ge(y_stored, 16 * JQ)

        @block.gpsimd
        def _(pool):
            nc.gpsimd.memset(ident[:], 0.0).then_inc(consts, 1)
            nc.gpsimd.memset(ones, 1.0).then_inc(consts, 1)
            nc.gpsimd.iota(iota_b[:], [[1, QWIN], [0, G]], 0, 0, allow_small_or_imprecise_dtypes=True)\
                .then_inc(consts, 1)
            nc.gpsimd.iota(round_no, [[1, MAXR]], 0, 0, allow_small_or_imprecise_dtypes=True).then_inc(consts, 1)
            pool.wait_ge(consts, 4)
            nc.gpsimd.affine_select(out=ident[:], in_=ident[:], compare_op=ALU.not_equal, fill=1.0, base=0,
                                    pattern=[[-1, P]], channel_multiplier=1).then_inc(ident_ready, 1)
            pool.wait_ge(ident_ready, 1)
            nc.gpsimd.tensor_copy(ident_b[:], ident[:]).then_inc(ident_ready, 1)
            nc.gpsimd.memset(counts[:], 0.0).then_inc(tail_zero, 1)

            for c in range(NLN):
                mine = slice(c * LNC, c * LNC + LNP)
                pool.wait_ge(ln_aggr, c + 1)
                for jj in range(c * LNC, c * LNC + LNP):
                    last = nc.gpsimd.tensor_scalar(rows[0:NP, jj, :], rows[0:NP, jj, :], meanvar[0:NP, jj, 0:1],
                                                   0.0, ALU.subtract, ALU.max)
                last.then_inc(ln_relu, 1)
                pool.wait_ge(ln_rstd, c + 1)
                pool.wait_ge(ln_relu, c + 1)
                nc.gpsimd.tensor_tensor(rows[0:NP, mine, :], rows[0:NP, mine, :],
                                        rstd[0:NP, mine].unsqueeze(2).to_broadcast([NP, LNP, D]),
                                        ALU.mult).then_inc(ln_pool, 1)
                if c == 0:
                    pool.wait_ge(src_in, 48)
                    nc.gpsimd.tensor_copy(src_f, src_i).then_inc(lists_f, 1)
                    pool.wait_ge(rel_in, 48)
                    nc.gpsimd.tensor_copy(rel_f, rel_i).then_inc(lists_f, 1)
            pool.wait_ge(rounds_ready, 1)
            rounds = pool.value_load(nrounds_i[0:1, 0:1], min_val=1, max_val=MAXR)

            def gathers(L, table, stored, n_stored):
                pool.wait_ge(stored, n_stored)
                width, in_loop, rest = bodies(L)
                with pool.Fori(0, rounds) as k:
                    def gather(u, t, gathered):
                        nc.gpsimd.indirect_dma_start(
                            L["slots"][u][:, t, :], None, table,
                            bass.IndirectOffsetOnAxis(ap=staged[:, u, t:t + 1], axis=0),
                        ).then_inc(gathered, 16)

                    def body(i, last):
                        for u in range(rest if last else width):
                            if u == RING:
                                pool.wait_ge(hT_turned, JQ)
                            if u == 2 * RING - 1:
                                pool.wait_ge(root_done, 1)
                            pool.wait_ge(L["idx_staged"][u], use_of_slot(L, u, k, i))
                            pool.sem_inc(L["begun"], 1)
                            if last and u == rest - 1:
                                for c in range(QG):
                                    for t in last_quads[c]:
                                        gather(u, t, L["last_quad"][c])
                            else:
                                for t in range(G):
                                    gather(u, t, L["gathered"][u])

                    with pool.Fori(0, in_loop) as i:
                        body(i, False)
                    body(in_loop, True)

            gathers(L1, table1, h_stored, 16 * NLN)
            gathers(L2, table2, h1_stored, 16 * JQ)

        @block.scalar
        def _(act):
            for L in (L1, L2):
                act.sem_inc(L["z_evac"], Z_BANKS)
            act.sem_inc(L1["t_evac"], SEED)
            act.sem_inc(root_out, SEED)
            for c in range(NLN):
                act.dma_start(rows[0:NP, c * LNC:(c + 1) * LNC, :],
                              rows_of(x)[:, c * LNC:(c + 1) * LNC, :]).then_inc(x_in[c], 16)

            def stage(L, u, col):
                act.wait_ge(tabs, 1)
                nc.scalar.copy(staged[:, u, :], src_tab[:, ds(col, G)]).then_inc(L["idx_staged"][u], 1)

            def hT_out(q):
                nj = min(4, NJ - 4 * q)
                act.wait_ge(hT_turned, q + 1)
                nc.scalar.copy(node_cols(h_T, 4 * q, nj),
                               bank(6 + q % 2, nj * NP).rearrange("h (j p) -> h j p", p=NP)).then_inc(hT_made, 1)

            hT_done = 0
            for c in range(NLN):
                j = slice(c * LNC, (c + 1) * LNC)
                act.wait_ge(ln_var, c + 1)
                nc.scalar.activation(std[0:NP, j], std[0:NP, j], ACT.Sqrt).then_inc(ln_std, 1)
                act.wait_ge(ln_scale, c + 1)
                for jj in range(c * LNC + LNP, (c + 1) * LNC):
                    last = nc.scalar.activation(rows[0:NP, jj, :], rows[0:NP, jj, :], ACT.Relu,
                                                bias=shift[0:NP, jj:jj + 1], scale=rstd[0:NP, jj:jj + 1])
                last.then_inc(ln_act, 1)
                if c == 2:
                    act.wait_ge(turned, 2)
                    nc.scalar.copy(src_tab[:], bank(0, NT)).then_inc(tabs, 1)
                    nc.scalar.copy(rel_b[:], bank(2, NT)).then_inc(tabs, 1)
                if c == 3:
                    act.wait_ge(turned, 3)
                    nc.scalar.copy(dl_tab[:], bank(4, NT)).then_inc(row_out, 1)
                if c >= 3:
                    while 4 * hT_done + 4 <= c * LNC:
                        hT_out(hT_done)
                        hT_done += 1
            for u in range(RING):
                stage(L1, u, u * G)
            for q in range(hT_done, JQ):
                hT_out(q)
            for u in range(RING, 2 * RING):
                stage(L1, u, u * G)

            def root_to_out(layer, chunk, made, went, n_made):
                act.wait_ge(made, n_made)
                nc.scalar.activation(out_T[:, chunk[0]:chunk[1]], chunk[2], ACT.Identity,
                                     bias=biases[:, layer:layer + 1]).then_inc(went, 1)

            def spread_rel(L, p, quads=range(QG)):
                if quads[0] == 0:
                    act.wait_ge(L["pick_made"], p * QG + SEED)
                for c in quads:
                    act.wait_ge(L["t_made"], p * QG + (c + 1 + SEED))
                    nc.scalar.copy(rel_T[:, c * QUAD:(c + 1) * QUAD, :].rearrange("r t e -> r (t e)"),
                                   bank(T_BANK, QUAD * P)).then_inc(L["t_evac"], 1)

            spread_rel(L1, 0)
            act.wait_ge(small_in, 64)
            act.wait_ge(rounds_ready, 1)
            rounds = act.value_load(nrounds_i[0:1, 0:1], min_val=1, max_val=MAXR)
            qrounds = act.value_load(nrounds_i[0:1, 1:2], min_val=1, max_val=MAXR)
            with act.Fori(0, qrounds) as k:
                for c in range(NCH):
                    at = min(c * BANK, N - BANK)
                    root_to_out(0, (at, at + BANK, bank(AUX_BANK)), root_made, root_out, k * NCH + (c + 1))
            act.wait_ge(root_out, qrounds * NCH + SEED)
            act.sem_inc(root_done, 1)

            def layer(L, first):
                width, in_loop, rest = bodies(L)
                with act.Fori(0, rounds) as k:
                    if first:
                        spread_rel(L, k * NG + 1)

                    def body(i, last):
                        for u in range(rest if last else width):
                            g = k * NG + i * width + u
                            ahead = first and not (last and u >= rest - 2)
                            for j in range(G // 2):
                                if ahead and j == T_AT:
                                    spread_rel(L, g + 2, range(1))
                                act.wait_ge(L["z_made"], g * (G // 2) + (j + 1))
                                n = min(2, REAL - 2 * j) if last and u == rest - 1 else 2
                                nc.scalar.copy(
                                    z_sb[:, :, 2 * j:2 * j + n, :].rearrange("h r t n -> h t r n"),
                                    bank(Z_BANK + j % Z_BANKS, n * R * WIN).rearrange("h (t r n) -> h t r n", t=n, r=R),
                                ).then_inc(L["z_evac"], 1)
                            if ahead:
                                spread_rel(L, g + 2, range(1, QG))
                            if last:
                                stage(L, u, u * G)
                            elif u < rest:
                                stage(L, u, i * (width * G) + (width + u) * G)
                            else:
                                stage(L, u, ((i + 1) % in_loop) * (width * G) + u * G)

                    with act.Fori(0, in_loop) as i:
                        body(i, False)
                    body(in_loop, True)
                    if first:
                        with act.If_lt(act.to_reg(k + 1), act.to_reg(rounds)):
                            spread_rel(L, k * NG + NG)

            layer(L1, True)
            for q in range(0, JQ, 2):
                nj = min(4, NJ - 4 * q)
                act.wait_ge(h1_turned, q + 1)
                nc.scalar.activation(rows[0:NP, 4 * q:4 * q + nj, :].rearrange("p j d -> p (j d)"),
                                     bank(q % 4, nj * D, NP), ACT.Relu).then_inc(h1_act, 1)
            for u in range(RING):
                stage(L2, u, u * G)
            for c in range(NCH):
                at = c * BANK
                n = min(BANK, N - at)
                root_to_out(1, (at, at + n, bank(c % 4, n)), root2_made, root2_out, c + 1)
            layer(L2, False)

        @block.vector
        def _(dve):
            dve.sem_inc(q_added, SEED)
            for s in [L[n] for L in (L1, L2) for n in ("added", "s_made")]:
                dve.sem_inc(s, SEED)
            dve.sem_inc(L1["node_c_made"], SEED_C)
            nc.vector.memset(dst_i[:, CH - 1, :], 0).then_inc(pads_set, 1)
            nc.vector.memset(src_i[:, CH - 1, :], 0).then_inc(pads_set, 1)
            nc.vector.memset(rel_i[:, CH - 1, :], -1).then_inc(pads_set, 1)
            nc.vector.memset(out_T[:, N:COLS], 0.0).then_inc(tail_zero, 1)

            def node_columns():
                dve.wait_ge(dst_in, 96)
                nc.vector.tensor_copy(dst_f, dst_i).then_inc(prep, 1)
                dve.wait_ge(prep, 1)
                nc.vector.tensor_reduce(dmin[:], dst_f, AX.X, ALU.min).then_inc(prep, 1)
                nc.vector.tensor_reduce(dmax[:], dst_f, AX.X, ALU.max).then_inc(prep, 1)
                dve.wait_ge(prep, 2)
                nc.vector.tensor_tensor(dl_f, dst_f, dmin[:].unsqueeze(2).to_broadcast([P, CH, P]),
                                        ALU.subtract).then_inc(dl_ready, 1)
                dve.wait_ge(prep, 3)
                nc.vector.tensor_tensor(tile_span[:], dmax[:], dmin[:], ALU.subtract).then_inc(prep, 1)
                dve.wait_ge(prep, 4)
                nc.vector.tensor_reduce(part_span[:], tile_span[:], AX.X, ALU.max).then_inc(prep, 1)

            for c in range(NLN + 1):
                if c < NLN:
                    dve.wait_ge(x_in[c], 16)
                    for jj in range(c * LNC, (c + 1) * LNC):
                        last = nc.vector.bn_stats(stats[0:NP, jj, :], rows[0:NP, jj, :])
                    last.then_inc(ln_stats, 1)
                    dve.wait_ge(ln_stats, c + 1)
                    for jj in range(c * LNC, (c + 1) * LNC):
                        last = nc.vector.bn_aggr(meanvar[0:NP, jj, :], stats[0:NP, jj, :])
                    last.then_inc(ln_aggr, 1)
                    dve.wait_ge(ln_aggr, c + 1)
                    j = slice(c * LNC, (c + 1) * LNC)
                    nc.vector.tensor_scalar(std[0:NP, j], meanvar[0:NP, j, 1], EPS, None, ALU.add).then_inc(ln_var, 1)
                if c > 0:
                    j = slice((c - 1) * LNC, c * LNC)
                    dve.wait_ge(ln_std, c)
                    nc.vector.reciprocal(rstd[0:NP, j], std[0:NP, j]).then_inc(ln_rstd, 1)
                    dve.wait_ge(ln_rstd, c)
                    nc.vector.scalar_tensor_tensor(out=shift[0:NP, j], in0=meanvar[0:NP, j, 0], scalar=-1.0,
                                                   in1=rstd[0:NP, j], op0=ALU.mult, op1=ALU.mult).then_inc(ln_scale, 1)
                if c == 1:
                    node_columns()
            quads = lambda a: a.rearrange("o (q t) -> o q t", t=QUAD)
            dve.wait_ge(turned, 4)
            nc.vector.tensor_copy(base_f[:], ps[0:1, 0:NT]).then_inc(base_out, 1)
            nc.vector.tensor_reduce(qmin, quads(ps[0:1, 0:NT]), AX.X, ALU.min).then_inc(base_out, 1)
            dve.wait_ge(turned, 5)
            nc.vector.tensor_reduce(qmax, quads(ps[0:1, 2 * BANK:2 * BANK + NT]), AX.X, ALU.max).then_inc(base_out, 1)
            dve.wait_ge(base_out, 2)
            nc.vector.tensor_tensor(quads(delta), quads(base_f[:]), qmin.unsqueeze(2).to_broadcast([1, NQ, QUAD]),
                                    ALU.subtract).then_inc(delta_ready, 1)
            dve.wait_ge(base_out, 3)
            nc.vector.tensor_tensor(qmax, qmax, qmin, ALU.subtract).then_inc(base_out, 1)
            nc.vector.tensor_reduce(spans[:, 0:1], ps[0:1, 4 * BANK - P:4 * BANK], AX.X, ALU.max)\
                .then_inc(base_out, 1)
            dve.wait_ge(base_out, 4)
            nc.vector.tensor_reduce(spans[:, 1:2], qmax, AX.X, ALU.max).then_inc(base_out, 1)
            dve.wait_ge(consts, 4)
            dve.wait_ge(base_out, 5)
            nc.vector.tensor_scalar(round_on, round_no, float(WIN), spans[:, 0:1], ALU.mult,
                                    ALU.is_le).then_inc(base_out, 1)
            dve.wait_ge(base_out, 6)
            nc.vector.tensor_scalar(round_on_q, round_no[:, 0:QMAXR], float(QWIN), spans[:, 1:2], ALU.mult,
                                    ALU.is_le).then_inc(base_out, 1)
            dve.wait_ge(base_out, 7)
            nc.vector.tensor_reduce(nrounds_f[:, 0:1], round_on, AX.X, ALU.add).then_inc(base_out, 1)
            dve.wait_ge(base_out, 8)
            nc.vector.tensor_reduce(nrounds_f[:, 1:2], round_on_q, AX.X, ALU.add).then_inc(base_out, 1)
            dve.wait_ge(base_out, 10)
            nc.vector.tensor_copy(nrounds_i[:], nrounds_f[:]).then_inc(rounds_ready, 1)
            dve.wait_ge(delta_spread, 1)
            dve.wait_ge(row_out, 1)
            nc.vector.tensor_tensor(dlq_tab[:], dl_tab[:], bank(0, NT), ALU.add).then_inc(base_out, 1)
            dve.wait_ge(base_out, 11)
            nc.vector.tensor_copy(dlq_b[:], dlq_tab[:]).then_inc(q_base, 1)
            nc.vector.tensor_scalar(qbase_i, qmin, float(QCOLS - QWIN), None, ALU.min).then_inc(q_base, 1)
            dve.wait_ge(rounds_ready, 1)
            rounds = dve.value_load(nrounds_i[0:1, 0:1], min_val=1, max_val=MAXR)
            qrounds = dve.value_load(nrounds_i[0:1, 1:2], min_val=1, max_val=MAXR)
            dve.wait_ge(tabs, 2)

            def hots_of(hot, b, table, col, width):
                return nc.vector.tensor_tensor(hot[:, b, 0:width, :], iota_b[:, 0:width, :],
                                               table[:, ds(col, G)].unsqueeze(1).to_broadcast([P, width, G]),
                                               ALU.is_equal)

            def layer_steps(L, first):
                nc.vector.memset(win_at[:], 0.0).then_inc(L["base_next"], 1)

                def place_windows(n):
                    dve.wait_ge(L["base_next"], n)
                    nc.vector.tensor_scalar(dl_b[:], dl_tab[:], win_at[:], None, ALU.subtract)
                    nc.vector.tensor_scalar(base_i[:], base_f[:], win_at[0:1, :], float(COLS - WIN), ALU.add, ALU.min)\
                        .then_inc(L["base_ready"], 1)

                place_windows(1)

                def hots(p, b, col):
                    hots_of(hot_node, b, dl_b, col, WIN)
                    hots_of(hot_rel, b, rel_b, col, RELP if first else R).then_inc(L["hot_made"], 1)
                    if first:
                        dve.wait_ge(L["hot_made"], p + 1)
                        dve.wait_ge(L["t_made"], p * QG + SEED)
                        nc.vector.tensor_copy(hot_rel_4[:], hot_rel[:, b, :, :].unsqueeze(1)
                                              .to_broadcast([P, QG, RELP, G])).then_inc(L["hot_4_made"], 1)

                def weighted(p, b, col, before):
                    if first:
                        dve.wait_ge(L["pick_made"], p * QG + (QG + SEED))
                        nc.vector.tensor_tensor(node_c[:], hot_node[:, b, :, :].rearrange("p n t -> p t n")
                                                .unsqueeze(3).to_broadcast([P, G, WIN, 2]),
                                                bank(PICK_BANK + b, G * WIN * 2)
                                                .rearrange("p (t n s) -> p t n s", n=WIN, s=2),
                                                ALU.mult).then_inc(L["node_c_made"], 1)
                        dve.wait_ge(L["node_c_made"], p + (1 + SEED_C))
                        nc.vector.tensor_reduce(count_part[:], node_c[:].rearrange("p t n s -> p t (n s)"), AX.X,
                                                ALU.add).then_inc(L["count_sum"], 1)
                        dve.wait_ge(L["count_sum"], p + 1)
                        nc.vector.tensor_tensor(count_tab[:, ds(col, G)], count_tab[:, ds(col, G)], count_part[:],
                                                ALU.add).then_inc(L["count_added"], 1)
                        dve.wait_ge(L["count_added"], p + 1)
                        nc.vector.tensor_scalar(count_or_1[:], count_tab[:, ds(col, G)], 1.0, None, ALU.max)\
                            .then_inc(L["count_max"], 1)
                        dve.wait_ge(L["count_max"], p + 1)
                        nc.vector.reciprocal(w_tab[:, ds(col, G)], count_or_1[:]).then_inc(L["w_made"], 1)
                        dve.wait_ge(L["w_made"], p + 1)
                    else:
                        dve.wait_ge(L["hot_made"], p + 1)
                    nc.vector.tensor_tensor(node_w[:], hot_node[:, b, :, :],
                                            w_tab[:, ds(col, G)].unsqueeze(1).to_broadcast([P, WIN, G]),
                                            ALU.mult).then_inc(L["node_w_made"], 1)
                    dve.wait_ge(L["node_w_made"], p + 1)
                    for h in range(2):
                        if before is not None:
                            dve.wait_ge(L["z_made"], before * (G // 2) + (h + 1) * (G // 4))
                        t = slice(h * G // 2, (h + 1) * G // 2)
                        nc.vector.tensor_tensor(
                            onehot_w[:, t, :, :],
                            hot_rel[:, b, 0:R, t].rearrange("p r t -> p t r").unsqueeze(3)
                            .to_broadcast([P, G // 2, R, WIN]),
                            node_w[:, :, t].rearrange("p n t -> p t n").unsqueeze(2).to_broadcast([P, G // 2, R, WIN]),
                            ALU.mult).then_inc(L["s_made"], 1)

                return place_windows, hots, weighted

            l1_steps = layer_steps(L1, True)
            dve.wait_ge(L1["base_ready"], 1)
            l1_steps[1](0, 0, 0)
            l1_steps[1](1, 1, G)

            def quad_hots(b, col):
                hots_of(hot_quad_rel, b, rel_b, col, R)
                hots_of(hot_quad, b, dlq_b, col, QWIN).then_inc(q_hot, 1)

            with dve.Fori(0, qrounds) as k:
                dve.wait_ge(q_base, k * 2 + 2)
                quad_hots(0, 0)
                quad_hots(1, G)

                def count_body(i, last):
                    for u in range(QB):
                        g = k * NG + i * QB + u
                        if not (last and u >= QB - 2):
                            quad_hots((u + 2) % QB, i * (QB * G) + (u + 2) * G)
                        dve.wait_ge(tail_zero, 2)
                        _, at = nc.values_load_multi_w_load_instructions(
                            qbase_i[0:1, ds(i * (QB * QG) + u * QG, QG)], engines=[mybir.EngineType.DVE],
                            min_val=0, max_val=QCOLS - QWIN,
                            skip_runtime_bounds_check_because="the row was clamped to its bounds when it was written")
                        dve.wait_ge(q_added, g * QG + SEED)
                        dve.wait_ge(q_counted, g + 1)
                        for c in range(QG):
                            nc.vector.tensor_tensor(
                                counts[c * RELP:c * RELP + R, ds(at[c], QWIN)],
                                counts[c * RELP:c * RELP + R, ds(at[c], QWIN)],
                                ps[c * RELP:c * RELP + R, u * BANK:u * BANK + QWIN],
                                ALU.add).then_inc(q_added, 1)

                with dve.Fori(0, NI - 1) as i:
                    count_body(i, False)
                count_body(NI - 1, True)
                nc.vector.tensor_scalar(dlq_tab[:], dlq_tab[:], float(-QWIN), None, ALU.add).then_inc(q_next, 1)
                nc.vector.tensor_scalar(qmin, qmin, float(QWIN), None, ALU.add).then_inc(q_next, 1)
                dve.wait_ge(q_next, k * 2 + 2)
                nc.vector.tensor_copy(dlq_b[:], dlq_tab[:]).then_inc(q_base, 1)
                nc.vector.tensor_scalar(qbase_i, qmin, float(QCOLS - QWIN), None, ALU.min).then_inc(q_base, 1)
            dve.wait_ge(q_added, qrounds * (NG * QG) + SEED)
            dve.wait_ge(q_base, qrounds * 2 + 2)
            nc.vector.tensor_tensor(count_lo, counts[:], count_hi, ALU.subtract).then_inc(counts_made, 1)
            nc.vector.memset(count_tab[:], 0.0).then_inc(tab_zero, 1)
            dve.wait_ge(tab_zero, 1)

            def layer(L, first, steps):
                place_windows, hots, weighted = steps
                width, in_loop, rest = bodies(L)
                with dve.Fori(0, rounds) as k:
                    if not first:
                        dve.wait_ge(L["base_ready"], k + 1)
                        dve.wait_ge(L["s_made"], k * (2 * NG) + SEED)
                        hots(k * NG, 0, 0)
                        hots(k * NG + 1, 1, G)
                    weighted(k * NG, 0, 0, None)
                    dve.wait_ge(L["s_made"], k * (2 * NG) + (2 + SEED))
                    hots(k * NG + 2, 0, 2 * G)

                    def body(i, last):
                        for u in range(rest if last else width):
                            g = k * NG + i * width + u
                            col = i * (width * G) + u * G
                            if not (last and u == rest - 1):
                                weighted(g + 1, (u + 1) % 2, col + G, g)
                            if not (last and u >= rest - 3):
                                dve.wait_ge(L["s_made"], g * 2 + (4 + SEED))
                                hots(g + 3, (u + 1) % 2, col + 3 * G)
                            dve.wait_ge(tail_zero, 2)
                            _, at = nc.values_load_multi_w_load_instructions(
                                base_i[0:1, ds(col, G)], engines=[mybir.EngineType.DVE],
                                min_val=0, max_val=COLS - WIN,
                                skip_runtime_bounds_check_because="the row was clamped to its bounds when written")
                            final = last and u == rest - 1
                            if not final:
                                dve.wait_ge(L["rel_made"], g + 1)
                            for t in range(REAL if final else G):
                                b = REL_BANK
                                if final and t == 0:
                                    dve.wait_ge(L["rel_first"], k + 1)
                                if final and t >= G // 2:
                                    b = T_BANK
                                    if t == G // 2:
                                        dve.wait_ge(L["rel_made"], g + 1)
                                dve.wait_ge(L["added"], g * G + (t + SEED))
                                nc.vector.tensor_tensor(
                                    out_T[:, ds(at[t], WIN)], out_T[:, ds(at[t], WIN)],
                                    bank(b)[:, t * WIN:(t + 1) * WIN],
                                    ALU.add).then_inc(L["added"], 1 + G - REAL if final and t == REAL - 1 else 1)

                    with dve.Fori(0, in_loop) as i:
                        body(i, False)
                    body(in_loop, True)
                    nc.vector.tensor_scalar(win_at[:], win_at[:], float(WIN), None, ALU.add)\
                        .then_inc(L["base_next"], 1)
                    place_windows(k + 2)
                    if first:
                        with dve.If_lt(dve.to_reg(k + 1), dve.to_reg(rounds)):
                            dve.wait_ge(L["base_ready"], k + 2)
                            dve.wait_ge(L["s_made"], (k + 1) * (2 * NG) + SEED)
                            hots(k * NG + NG, 0, 0)
                            hots(k * NG + NG + 1, 1, G)

            dve.wait_ge(root_done, 1)
            layer(L1, True, l1_steps)
            for q in range(1, JQ, 2):
                nj = min(4, NJ - 4 * q)
                dve.wait_ge(h1_turned, q + 1)
                nc.vector.tensor_scalar(rows[0:NP, 4 * q:4 * q + nj, :].rearrange("p j d -> p (j d)"),
                                        bank(q % 4, nj * D, NP), 0.0, None, ALU.max).then_inc(h1_dve, 1)
            dve.wait_ge(L1["added"], rounds * (NG * G) + SEED)
            nc.vector.tensor_scalar(h_T[:], out_T[:, 0:N], 0.0, None, ALU.max).then_inc(h1T_made, 1)
            dve.wait_ge(root2_out, NCH)
            layer(L2, False, layer_steps(L2, False))
            dve.wait_ge(x_again, 16)
            for q in range(JQ):
                nj = min(4, NJ - 4 * q)
                r = rows[0:NP, 4 * q:4 * q + nj, :].rearrange("p j d -> p (j d)")
                dve.wait_ge(y_turned, q + 1)
                nc.vector.tensor_tensor(r, r, bank(q % 4, nj * D, NP), ALU.add).then_inc(y_made, 1)

        @block.tensor
        def _(pe):
            pe.sem_inc(L1["pick_made"], SEED)
            pe.sem_inc(L1["t_made"], SEED)
            pe.wait_ge(ident_ready, 2)
            for n, (a, s, need, b) in enumerate(((src_f, lists_f, 1, 0), (rel_f, lists_f, 2, 2), (dl_f, dl_ready, 1, 4))):
                pe.wait_ge(s, need)
                for c in range(CH):
                    w = min(P, NT - c * P)
                    last = nc.tensor.transpose(ps[:, b * BANK + c * P:b * BANK + c * P + w], a[0:w, c, :],
                                               ident[0:w, 0:w])
                last.then_inc(turned, 1)

            def row_of(col, b, more=None):
                for c in range(CH):
                    last = nc.tensor.transpose(ps[0:1, b * BANK + c * P:b * BANK + (c + 1) * P], col[:, c:c + 1],
                                               ident[:])
                if more is not None:
                    last = nc.tensor.transpose(ps[0:1, (b + 2) * BANK - P:(b + 2) * BANK], more[:], ident[:])
                last.then_inc(turned, 1)

            def turn_h(q):
                nj = min(4, NJ - 4 * q)
                pe.wait_ge(ln_act, (4 * q + nj - 1) // LNC + 1)
                pe.wait_ge(ln_pool, (4 * q + nj - 1) // LNC + 1)
                if q >= 2:
                    pe.wait_ge(hT_made, q - 1)
                for j in range(nj):
                    last = nc.tensor.transpose(bank(6 + q % 2, 4 * NP)[:, j * NP:(j + 1) * NP],
                                               rows[0:NP, 4 * q + j, :], ident[0:NP, 0:NP])
                last.then_inc(hT_turned, 1)

            pe.wait_ge(tabs, 1)
            row_of(dmin, 0)
            pe.wait_ge(tabs, 2)
            pe.wait_ge(prep, 5)
            row_of(dmax, 2, part_span)
            for q in range(JQ - 3):
                turn_h(q)
            pe.wait_ge(consts, 4)
            pe.wait_ge(delta_ready, 1)
            for c in range(0, NT, BANK):
                n = min(BANK, NT - c)
                last = nc.tensor.matmul(bank(c // BANK, n), ones, delta[:, c:c + n], start=True, stop=True)
            last.then_inc(delta_spread, 1)
            for q in range(JQ - 3, JQ):
                turn_h(q)
            pe.wait_ge(rounds_ready, 1)
            rounds = pe.value_load(nrounds_i[0:1, 0:1], min_val=1, max_val=MAXR)
            qrounds = pe.value_load(nrounds_i[0:1, 1:2], min_val=1, max_val=MAXR)
            pe.wait_ge(row_out, 1)

            def rel_turn(L, p, c):
                if c == 0:
                    pe.wait_ge(L["hot_4_made"], p + 1)
                pe.wait_ge(L["t_evac"], p * QG + (c + SEED))
                for t in range(QUAD):
                    hot = hot_rel_4[:, :, :, c * QUAD + t].rearrange("p q r -> p (q r)")
                    last = nc.tensor.matmul(bank(T_BANK)[:, t * P:(t + 1) * P], hot, ident_b[:], start=True,
                                            stop=True)
                last.then_inc(L["t_made"], 1)

            for c in range(QG):
                rel_turn(L1, 0, c)
            pe.wait_ge(small_in, 64)
            pe.wait_ge(hT_made, JQ)
            with pe.Fori(0, qrounds) as k:
                def count_body(i, last_body):
                    for u in range(QB):
                        g = k * NG + i * QB + u
                        pe.wait_ge(q_hot, g + 1)
                        for t in range(G):
                            c = t // QUAD
                            last = nc.tensor.matmul(
                                ps[c * RELP:c * RELP + R, u * BANK:u * BANK + QWIN],
                                hot_quad_rel[:, u, :, t], hot_quad[:, u, :, t], start=t % QUAD == 0,
                                stop=t % QUAD == QUAD - 1)
                        last.then_inc(q_counted, 1)
                    pe.wait_ge(root_out, k * NCH + (i + SEED))
                    h_cols = h_T[:, N - BANK:N] if last_body else h_T[:, ds(i * BANK, BANK)]
                    nc.tensor.matmul(bank(AUX_BANK), roots[:, 0, :], h_cols, start=True,
                                     stop=True).then_inc(root_made, 1)

                with pe.Fori(0, NI - 1) as i:
                    count_body(i, False)
                count_body(NI - 1, True)
            pe.wait_ge(w_in, 16 * R)
            pe.wait_ge(root_done, 1)

            def pick(L, p, b, c, at):
                if c == 0:
                    pe.wait_ge(L["node_c_made"], p + (SEED_C - 1))
                pe.wait_ge(L["t_evac"], p * QG + (c + 1 + SEED))
                pe.wait_ge(counts_made, 1)
                for t in range(c * QUAD, (c + 1) * QUAD):
                    last = nc.tensor.matmul(bank(PICK_BANK + b)[:, t * 2 * WIN:(t + 1) * 2 * WIN],
                                            rel_T[:, t, :], halves[:, ds(at[t] * 2, 2 * WIN)], start=True, stop=True)
                last.then_inc(L["pick_made"], 1)

            def windows(col):
                return nc.values_load_multi_w_load_instructions(
                    base_i[0:1, ds(col, G)], engines=[mybir.EngineType.PE], min_val=0, max_val=COLS - WIN,
                    skip_runtime_bounds_check_because="the row was clamped to its bounds when it was written")[1]

            def layer(L, first):
                width, in_loop, rest = bodies(L)
                with pe.Fori(0, rounds) as k:
                    if first:
                        for p in range(2):
                            for c in range(QG):
                                if p > 0:
                                    rel_turn(L, k * NG + p, c)
                                if c == 0:
                                    at = windows(p * G)
                                pick(L, k * NG + p, p, c, at)

                    def body(i, last):
                        for u in range(rest if last else width):
                            g = k * NG + i * width + u
                            ahead = first and not (last and u >= rest - 2)
                            if ahead:
                                at = windows(i * (width * G) + (u + 2) * G)
                            final = last and u == rest - 1
                            if not final:
                                pe.wait_ge(L["gathered"][u], fills_of_slot(L, u, k, i) * (16 * G))

                            def relations(b, tiles, made):
                                for r in range(R):
                                    mm = nc.tensor.matmul(
                                        bank(b)[:, tiles.start * WIN:tiles.stop * WIN], wrel[:, r, :],
                                        z_sb[:, r, tiles, :].rearrange("h t n -> h (t n)"),
                                        start=(r == 0), stop=(r == R - 1))
                                    if ahead and r in PICKS_AT:
                                        c = PICKS_AT.index(r) + 1
                                        pick(L, g + 2, u % 2, c, at)
                                        if c < QG - 1:
                                            rel_turn(L, g + 2, c + 1)
                                mm.then_inc(made, 1)

                            for j in range(G // 2):
                                if ahead and j == T_AT:
                                    rel_turn(L, g + 2, 0)
                                if j % (G // 4) == 0:
                                    pe.wait_ge(L["s_made"], g * 2 + (j // (G // 4) + 1 + SEED))
                                if final and j % 2 == 0:
                                    pe.wait_ge(L["last_quad"][j // 2], (k + 1) * (16 * len(last_quads[j // 2])))
                                pe.wait_ge(L["z_evac"], g * (G // 2) + (j + 1))
                                for t in range(2 * j, min(2 * j + 2, REAL) if final else 2 * j + 2):
                                    mm = nc.tensor.matmul(
                                        bank(Z_BANK + j % Z_BANKS, 2 * R * WIN)[:, t % 2 * R * WIN:(t % 2 + 1) * R * WIN],
                                        L["slots"][u][:, t, :], onehot_w[:, t, :, :].rearrange("p r n -> p (r n)"),
                                        start=True, stop=True)
                                mm.then_inc(L["z_made"], 1)
                                if final and j == G // 2 - 3:
                                    pe.wait_ge(L["z_evac"], g * (G // 2) + (G // 4 + Z_BANKS))
                                    pe.wait_ge(L["added"], g * G + SEED)
                                    relations(REL_BANK, slice(0, G // 2), L["rel_first"])
                            if ahead:
                                pick(L, g + 2, u % 2, 0, at)
                                rel_turn(L, g + 2, 1)
                            pe.wait_ge(L["z_evac"], g * (G // 2) + (G // 2 + Z_BANKS))
                            if final:
                                relations(T_BANK, slice(G // 2, REAL), L["rel_made"])
                            else:
                                pe.wait_ge(L["added"], g * G + SEED)
                                relations(REL_BANK, slice(0, G), L["rel_made"])

                    with pe.Fori(0, in_loop) as i:
                        body(i, False)
                    body(in_loop, True)
                    if first:
                        with pe.If_lt(pe.to_reg(k + 1), pe.to_reg(rounds)):
                            for c in range(QG):
                                rel_turn(L, k * NG + NG, c)

            def out_rows(L, turned_s, ready):
                pe.wait_ge(L["added"], rounds * (NG * G) + SEED)
                for q in range(JQ):
                    nj = min(4, NJ - 4 * q)
                    if q >= 4:
                        ready(q)
                    for j in range(nj):
                        mm = nc.tensor.transpose(bank(q % 4, BANK, NP)[:, j * D:(j + 1) * D],
                                                 node_cols(out_T, 4 * q + j, 1).rearrange("h j p -> h (j p)"),
                                                 ident[:])
                    mm.then_inc(turned_s, 1)

            layer(L1, True)
            out_rows(L1, h1_turned, lambda q: pe.wait_ge(h1_dve if q % 2 else h1_act, (q - 4) // 2 + 1))
            pe.wait_ge(h1_act, (JQ + 1) // 2)
            pe.wait_ge(h1_dve, JQ // 2)
            pe.wait_ge(h1T_made, 1)
            for c in range(NCH):
                n = min(BANK, N - c * BANK)
                if c >= 4:
                    pe.wait_ge(root2_out, c - 3)
                nc.tensor.matmul(bank(c % 4, n), roots[:, 1, :], h_T[:, c * BANK:c * BANK + n], start=True,
                                 stop=True).then_inc(root2_made, 1)
            pe.wait_ge(w2_in, 16 * R)
            pe.wait_ge(root2_out, NCH)
            layer(L2, False)
            out_rows(L2, y_turned, lambda q: pe.wait_ge(y_made, q - 3))


_INS = ["x", "src", "dst", "edge_type_16", "L0_gnn_W1", "L0_gnn_root1", "L0_gnn_b1", "L0_gnn_W2", "L0_gnn_root2",
        "L0_gnn_b2"]


def kernel(**inputs):
    import numpy as _np
    import concourse.bacc as _bacc
    from concourse import mybir as _mybir
    from concourse.bass_utils import run_bass_kernel_spmd as _run

    nc = _bacc.Bacc("TRN2", target_bir_lowering=False, num_devices=1)
    arrays, args = {}, []
    for name in _INS:
        a = _np.ascontiguousarray(inputs[name])
        arrays[f"in_{name}_dram"] = a
        args.append(nc.dram_tensor(f"in_{name}_dram", a.shape, _mybir.dt.from_np(a.dtype), kind="ExternalInput").ap())
    shape = inputs["x"].shape
    args.append(nc.dram_tensor("out_0_dram", shape, _mybir.dt.float32, kind="ExternalOutput").ap())
    rgcn_kernel(nc, *args)
    r = _run(nc, [arrays], core_ids=[0])
    return r.results[0]["out_0_dram"]
```

```python
from contextlib import ExitStack

import concourse.bass as bass
from concourse import mybir

F32 = mybir.dt.float32
BF16 = mybir.dt.bfloat16
I32 = mybir.dt.int32
ALU = mybir.AluOpType
ACT = mybir.ActivationFunctionType
AX = mybir.AxisListType
ds = bass.ds

P = 128
EPS = 1e-5
G = 16
RING = 4
WIN = 12
QUAD = 4
QWIN = 48
QB = 4
Z_BANKS = 4
SEED = 1
SEED_C = 2
HT_EARLY = 3
T_AT = 6
PICKS_AT = (3, 8, 13)
RELP = 32
BANK = 512


def rgcn_kernel(nc, x, src, dst, rel, w1, root1, b1, w2, root2, b2, out):
    N, D = x.shape
    E = src.shape[0]
    R = w1.shape[0]
    NT = -(-E // (P * G * RING)) * G * RING
    NG = NT // G
    NI = NG // RING
    REAL = -(-E // P) - (NG - 1) * G
    CH = -(-NT // P)
    FULL = E // P
    LAST = E - FULL * P
    NP = next(p for p in range(P, 0, -1) if N % p == 0)
    NJ = N // NP
    MAXR = -(-N // WIN)
    COLS = N + WIN + (-(N + WIN)) % 4
    QCOLS = N + QWIN + (-(N + QWIN)) % 4
    QG = G // QUAD
    assert QG * RELP == P and (QG - 1) * QUAD < REAL < G
    last_quads = [[range(c * QUAD, min((c + 1) * QUAD, tiles)) for c in range(QG)] for tiles in (G, REAL)]
    assert D == P and R <= RELP and FULL // P == CH - 1 and 0 < LAST < P and NT - FULL == 2
    LNC = 10
    LNP = 3
    NLN = NJ // LNC
    assert NJ % LNC == 0
    JQ = -(-NJ // 4)
    NCH = -(-N // BANK)
    assert NCH == NI and QB == RING and NJ >= G * (RING - 1)

    table1 = nc.dram_tensor("h_rows_dram", (N, D), F32).ap()
    table2 = nc.dram_tensor("h1_rows_dram", (N, D), F32).ap()
    rows_of = lambda a: a.rearrange("(p j) d -> p j d", j=NJ)

    with ExitStack() as ctx:
        def sb(name, shape, dt=F32):
            return ctx.enter_context(nc.sbuf_tensor(name, shape, dt))

        def sem(name):
            return ctx.enter_context(nc.semaphore(name))

        ps = ctx.enter_context(nc.psum_tensor("ps", [P, 8 * BANK], F32))
        Z_BANK, REL_BANK, T_BANK, PICK_BANK, AUX_BANK = 0, 4, 5, 6, 7

        def bank(b, n=BANK, parts=P):
            return ps[0:parts, b * BANK:b * BANK + n]

        rows = sb("rows", [P, NJ, D])
        h_T = sb("h_T", [P, N])
        out_T = sb("out_T", [P, COLS])
        wrel = sb("wrel", [P, R, D])
        roots = sb("roots", [P, 2, D])
        biases = sb("biases", [P, 2])
        ring = sb("ring", [P, RING, G, D])
        more_slots = [rows.rearrange("p j d -> p (j d)")[:, u * G * D:(u + 1) * G * D] for u in range(RING - 1)]\
            + [h_T[:, 0:G * D]]
        slots_2 = [ring[:, u] for u in range(RING)]
        slots_1 = slots_2 + [a.rearrange("p (t d) -> p t d", t=G) for a in more_slots]
        assert (NG % len(slots_1)) % 2 == 0 and NG % len(slots_2) == 0
        SN = G * R * WIN
        work = sb("work", [P, 2 * SN])
        onehot_w = work[:, 0:SN].rearrange("p (t r n) -> p t r n", t=G, r=R)
        z_sb = work[:, SN:2 * SN].rearrange("p (r t n) -> p r t n", t=G, r=R)
        CW = CH * P

        def list_rows(i):
            return work[:, i * CW:(i + 1) * CW].rearrange("p (c e) -> p c e", e=P)

        dst_i, src_i, rel_i = (list_rows(i).bitcast(I32) for i in range(3))
        dst_f, src_f, rel_f = (list_rows(i) for i in range(3))
        dl_f = list_rows(3)
        NQ = NT // QUAD
        QMAXR = -(-N // QWIN)
        at = 4 * CW

        def row(n):
            nonlocal at
            at += n
            assert at <= 2 * SN
            return work[0:1, at - n:at]

        delta, round_no, round_on_q, qmax = row(NT), row(MAXR), row(QMAXR), row(NQ)
        assert MAXR <= CW
        round_on = work[0:1, CW:CW + MAXR]
        src_tab = sb("src_tab", [P, NT])
        dl_tab = sb("dl_tab", [P, NT])
        dlq_tab = sb("dlq_tab", [P, NT])
        count_tab = dlq_tab
        w_tab = sb("w_tab", [P, NT])
        rel_b = sb("rel_b", [P, NT], BF16)
        dl_b = sb("dl_b", [P, NT], BF16)
        dlq_b = sb("dlq_b", [P, NT], BF16)
        counts = sb("counts", [P, QCOLS])
        hot_rel = sb("hot_rel", [P, 2, RELP, G], BF16)
        hot_node = sb("hot_node", [P, 2, WIN, G], BF16)
        hot_rel_4 = sb("hot_rel_4", [P, QG, RELP, G], BF16)
        assert NG * QUAD * P < 1 << 16
        halves = counts[:].bitcast(BF16)
        count_lo, count_hi = (halves.rearrange("p (n s) -> p n s", s=2)[:, :, i] for i in range(2))
        rel_T = sb("rel_T", [P, G, P], BF16)
        count_hots = work[:, 0:QB * (QWIN + R) * G // 2].bitcast(BF16)
        hot_quad = count_hots[:, 0:QB * QWIN * G].rearrange("p (b n t) -> p b n t", b=QB, t=G)
        hot_quad_rel = count_hots[:, QB * QWIN * G:].rearrange("p (b n t) -> p b n t", b=QB, t=G)
        q_rows = work[0:1, QB * (QWIN + R) * G // 2:3 * CW]
        assert q_rows.shape[1] >= 2 * NQ
        qmin = q_rows[:, 0:NQ]
        qbase_i = q_rows[:, NQ:2 * NQ].bitcast(I32)
        node_c = sb("node_c", [P, G, WIN, 2])
        node_w = sb("node_w", [P, WIN, G])
        count_part = sb("count_part", [P, G])
        count_or_1 = sb("count_or_1", [P, G])
        staged = sb("staged", [P, 2 * RING, G], I32)
        ident = sb("ident", [P, P])
        ident_b = sb("ident_b", [P, P], BF16)
        ones = hot_node[0:1].rearrange("p b n t -> p (b n t)").bitcast(F32)[:, 0:P]
        iota_b = sb("iota_b", [P, QWIN, G], BF16)
        dmin = sb("dmin", [P, CH])
        dmax = sb("dmax", [P, CH])
        base_f = sb("base_f", [1, NT])
        tile_span = sb("tile_span", [P, CH])
        part_span = sb("part_span", [P, 1])
        win_at = sb("win_at", [P, 1])
        base_i = sb("base_i", [1, NT], I32)
        spans = sb("spans", [1, 2])
        nrounds_f = sb("nrounds_f", [1, 2])
        nrounds_i = sb("nrounds_i", [1, 2], I32)
        stats = ring[:, 0, :, :].rearrange("p t d -> p (t d)")[:, 0:6 * NJ].rearrange("p (j s) -> p j s", s=6)
        ln_cols = ring[:, 1, 0:6, :].rearrange("p t d -> p (t d)")
        meanvar = ln_cols[:, 0:2 * NJ].rearrange("p (j s) -> p j s", s=2)
        std, rstd, shift = (ln_cols[:, n * NJ:(n + 1) * NJ] for n in (2, 3, 4))

        pads_set = sem("pads_set")
        dst_in, src_in, rel_in = sem("dst_in"), sem("src_in"), sem("rel_in")
        x_in = [sem(f"x_in{c}") for c in range(NLN)]
        w_in, small_in = sem("w_in"), sem("small_in")
        consts = sem("consts")
        ident_ready = sem("ident_ready")
        lists_f = sem("lists_f")
        dl_ready = sem("dl_ready")
        prep = sem("prep")
        turned = sem("turned")
        tabs = sem("tabs")
        base_out = sem("base_out")
        delta_ready = sem("delta_ready")
        delta_spread = sem("delta_spread")
        round_1, rounds_ready = sem("round_1"), sem("rounds_ready")
        ln_var = sem("ln_var")
        ln_std = sem("ln_std")
        ln_stats, ln_aggr, ln_rstd = sem("ln_stats"), sem("ln_aggr"), sem("ln_rstd")
        ln_scale = sem("ln_scale")
        ln_act, ln_pool = sem("ln_act"), sem("ln_pool")
        ln_relu = sem("ln_relu")
        h_stored = sem("h_stored")
        root_done = sem("root_done")
        row_out = sem("row_out")
        q_hot = sem("q_hot")
        q_counted = sem("q_counted")
        q_added = sem("q_added")
        q_base = sem("q_base")
        q_next = sem("q_next")
        counts_made = sem("counts_made")
        tab_zero = sem("tab_zero")
        hT_turned = sem("hT_turned")
        hT_made = sem("hT_made")
        root_made = sem("root_made")
        root_out = sem("root_out")
        tail_zero = sem("tail_zero")

        def layer_sems(n):
            names = ("begun base_next base_ready hot_made hot_4_made t_made t_evac pick_made node_c_made count_sum "
                     "count_added count_max w_made node_w_made s_made z_made z_evac rel_first rel_made added").split()
            d = {name: sem(f"{name}_{n}") for name in names}
            d["slots"] = slots_1 if n == 1 else slots_2
            d["idx_staged"] = [sem(f"idx_staged{u}_{n}") for u in range(len(d["slots"]))]
            d["gathered"] = [sem(f"gathered{u}_{n}") for u in range(len(d["slots"]))]
            d["last_quad"] = [[sem(f"last_quad{l}_{c}_{n}") for c in range(QG)] for l in range(2)]
            return d

        L1, L2 = layer_sems(1), layer_sems(2)
        w2_in = sem("w2_in")
        h1_turned, h1_act, h1_dve = sem("h1_turned"), sem("h1_act"), sem("h1_dve")
        h1_stored = sem("h1_stored")
        h1T_made = sem("h1T_made")
        root2_made, root2_out = sem("root2_made"), sem("root2_out")
        x_again = sem("x_again")
        y_turned, y_made, y_stored = sem("y_turned"), sem("y_made"), sem("y_stored")

        def bodies(L):
            width = len(L["slots"])
            in_loop = (NG - 1) // width
            return width, in_loop, NG - in_loop * width

        def use_of_slot(L, u, k, i):
            width, in_loop, rest = bodies(L)
            return k * (in_loop + (u < rest)) + i + 1

        def fills_of_slot(L, u, k, i):
            width, in_loop, rest = bodies(L)
            return k * (in_loop + (u < rest - 2)) + i + 1

        def node_cols(a, j0, nj):
            return a[:, 0:N].rearrange("h (p j) -> h j p", j=NJ)[:, j0:j0 + nj, :]

        block = ctx.enter_context(nc.Block())

        @block.sync
        def _(sp):
            whole = (CH - 1) * P * P
            left = FULL - (CH - 1) * P
            sp.wait_ge(pads_set, 3)
            for a, rows_i, s in ((dst, dst_i, dst_in), (src, src_i, src_in), (rel, rel_i, rel_in)):
                sp.dma_start(rows_i[:, 0:CH - 1, :], a[0:whole].rearrange("(c p e) -> p c e", p=P, e=P)).then_inc(s, 16)
                sp.dma_start(rows_i[0:left, CH - 1, :],
                             a[whole:FULL * P].rearrange("(p e) -> p e", e=P)).then_inc(s, 16)
                real = a[FULL * P:E].rearrange("(o e) -> o e", o=1)
                sp.dma_start(rows_i[left:left + 1, CH - 1, 0:LAST], real).then_inc(s, 16)
                if a is dst:
                    reps, rest = divmod(P - LAST, LAST)
                    pad = dst_i[left:left + 1, CH - 1, LAST:P]
                    sp.dma_start(pad[:, 0:reps * LAST].rearrange("o (r e) -> o r e", e=LAST),
                                 real.unsqueeze(1).to_broadcast([1, reps, LAST])).then_inc(s, 16)
                    sp.dma_start(pad[:, reps * LAST:], real[:, 0:rest]).then_inc(s, 16)
                    sp.dma_start(dst_i[left + 1:left + 2, CH - 1, :],
                                 dst[E - P:E].rearrange("(o e) -> o e", o=1)).then_inc(s, 16)
            sp.dma_start(roots[:, 0, :], root1).then_inc(small_in, 16)
            sp.dma_start(roots[:, 1, :], root2).then_inc(small_in, 16)
            sp.dma_start(biases[:, 0:1], b1.rearrange("(h o) -> h o", o=1)).then_inc(small_in, 16)
            sp.dma_start(biases[:, 1:2], b2.rearrange("(h o) -> h o", o=1)).then_inc(small_in, 16)
            for c in range(NLN):
                sp.wait_ge(ln_act, c + 1)
                sp.wait_ge(ln_pool, c + 1)
                sp.dma_start(rows_of(table1)[:, c * LNC:(c + 1) * LNC, :],
                             rows[0:NP, c * LNC:(c + 1) * LNC, :]).then_inc(h_stored, 16)
            for r in range(R):
                sp.dma_start(wrel[:, r, :], w1[r]).then_inc(w_in, 16)
            for q in range(JQ):
                nj = min(4, NJ - 4 * q)
                sp.wait_ge(h1_dve if q % 2 else h1_act, q // 2 + 1)
                sp.dma_start(rows_of(table2)[:, 4 * q:4 * q + nj, :],
                             rows[0:NP, 4 * q:4 * q + nj, :]).then_inc(h1_stored, 16)
            sp.wait_ge(h1_turned, 1)
            for r in range(R):
                sp.dma_start(wrel[:, r, :], w2[r]).then_inc(w2_in, 16)
            sp.wait_ge(h1_stored, 16 * JQ)
            sp.dma_start(rows[0:NP, :, :], rows_of(x)).then_inc(x_again, 16)
            for q in range(JQ):
                nj = min(4, NJ - 4 * q)
                sp.wait_ge(y_made, q + 1)
                sp.dma_start(rows_of(out)[:, 4 * q:4 * q + nj, :],
                             rows[0:NP, 4 * q:4 * q + nj, :]).then_inc(y_stored, 16)
            sp.wait_ge(y_stored, 16 * JQ)

        @block.gpsimd
        def _(pool):
            nc.gpsimd.memset(ident[:], 0.0).then_inc(consts, 1)
            nc.gpsimd.memset(ones, 1.0).then_inc(consts, 1)
            nc.gpsimd.iota(iota_b[:], [[1, QWIN], [0, G]], 0, 0, allow_small_or_imprecise_dtypes=True)\
                .then_inc(consts, 1)
            nc.gpsimd.iota(round_no, [[1, MAXR]], 0, 0, allow_small_or_imprecise_dtypes=True).then_inc(consts, 1)
            pool.wait_ge(consts, 4)
            nc.gpsimd.affine_select(out=ident[:], in_=ident[:], compare_op=ALU.not_equal, fill=1.0, base=0,
                                    pattern=[[-1, P]], channel_multiplier=1).then_inc(ident_ready, 1)
            pool.wait_ge(ident_ready, 1)
            nc.gpsimd.tensor_copy(ident_b[:], ident[:]).then_inc(ident_ready, 1)
            nc.gpsimd.memset(counts[:, QCOLS // 2:], 0.0).then_inc(tail_zero, 1)

            for c in range(NLN):
                mine = slice(c * LNC, c * LNC + LNP)
                pool.wait_ge(ln_aggr, c + 1)
                for jj in range(c * LNC, c * LNC + LNP):
                    last = nc.gpsimd.tensor_scalar(rows[0:NP, jj, :], rows[0:NP, jj, :], meanvar[0:NP, jj, 0:1],
                                                   0.0, ALU.subtract, ALU.max)
                last.then_inc(ln_relu, 1)
                pool.wait_ge(ln_rstd, c + 1)
                pool.wait_ge(ln_relu, c + 1)
                nc.gpsimd.tensor_tensor(rows[0:NP, mine, :], rows[0:NP, mine, :],
                                        rstd[0:NP, mine].unsqueeze(2).to_broadcast([NP, LNP, D]),
                                        ALU.mult).then_inc(ln_pool, 1)
            pool.wait_ge(prep, 3)
            nc.gpsimd.tensor_tensor(dl_f, dst_f, dmin[:].unsqueeze(2).to_broadcast([P, CH, P]),
                                    ALU.subtract).then_inc(dl_ready, 1)
            pool.wait_ge(rounds_ready, 1)
            rounds = pool.value_load(nrounds_i[0:1, 0:1], min_val=1, max_val=MAXR)

            def gathers(L, table, stored, n_stored):
                pool.wait_ge(stored, n_stored)
                width, in_loop, rest = bodies(L)
                with pool.Fori(0, rounds) as k:
                    def gather(u, t, gathered):
                        nc.gpsimd.indirect_dma_start(
                            L["slots"][u][:, t, :], None, table,
                            bass.IndirectOffsetOnAxis(ap=staged[:, u, t:t + 1], axis=0),
                        ).then_inc(gathered, 16)

                    def body(i, last):
                        for u in range(rest if last else width):
                            if u == RING:
                                pool.wait_ge(hT_turned, JQ)
                            if u == 2 * RING - 1:
                                pool.wait_ge(root_done, 1)
                            pool.wait_ge(L["idx_staged"][u], use_of_slot(L, u, k, i))
                            pool.sem_inc(L["begun"], 1)
                            if last and u >= rest - 2:
                                for c in range(QG):
                                    for t in last_quads[u - rest + 2][c]:
                                        gather(u, t, L["last_quad"][u - rest + 2][c])
                            else:
                                for t in range(G):
                                    gather(u, t, L["gathered"][u])

                    with pool.Fori(0, in_loop) as i:
                        body(i, False)
                    body(in_loop, True)

            gathers(L1, table1, h_stored, 16 * NLN)
            gathers(L2, table2, h1_stored, 16 * JQ)

        @block.scalar
        def _(act):
            for L in (L1, L2):
                act.sem_inc(L["z_evac"], Z_BANKS)
            act.sem_inc(L1["t_evac"], SEED)
            act.sem_inc(root_out, SEED)
            for c in range(NLN):
                act.dma_start(rows[0:NP, c * LNC:(c + 1) * LNC, :],
                              rows_of(x)[:, c * LNC:(c + 1) * LNC, :]).then_inc(x_in[c], 16)

            def stage(L, u, col):
                act.wait_ge(tabs, 1)
                nc.scalar.copy(staged[:, u, :], src_tab[:, ds(col, G)]).then_inc(L["idx_staged"][u], 1)

            def hT_out(q):
                nj = min(4, NJ - 4 * q)
                act.wait_ge(hT_turned, q + 1)
                nc.scalar.copy(node_cols(h_T, 4 * q, nj),
                               bank(2 + q % 2, nj * NP).rearrange("h (j p) -> h j p", p=NP)).then_inc(hT_made, 1)

            for c in range(NLN):
                j = slice(c * LNC, (c + 1) * LNC)
                act.wait_ge(ln_var, c + 1)
                nc.scalar.activation(std[0:NP, j], std[0:NP, j], ACT.Sqrt).then_inc(ln_std, 1)
                act.wait_ge(ln_scale, c + 1)
                for jj in range(c * LNC + LNP, (c + 1) * LNC):
                    last = nc.scalar.activation(rows[0:NP, jj, :], rows[0:NP, jj, :], ACT.Relu,
                                                bias=shift[0:NP, jj:jj + 1], scale=rstd[0:NP, jj:jj + 1])
                last.then_inc(ln_act, 1)
            act.wait_ge(turned, 2)
            nc.scalar.copy(src_tab[:], bank(0, NT)).then_inc(tabs, 1)
            nc.scalar.copy(rel_b[:], bank(2, NT)).then_inc(tabs, 1)
            for u in range(RING):
                stage(L1, u, u * G)
            for q in range(JQ):
                if q == 2:
                    act.wait_ge(turned, 6)
                    nc.scalar.copy(dl_tab[:], bank(6, NT)).then_inc(row_out, 1)
                hT_out(q)
            for u in range(RING, 2 * RING):
                stage(L1, u, u * G)

            def root_to_out(layer, chunk, made, went, n_made):
                act.wait_ge(made, n_made)
                nc.scalar.activation(out_T[:, chunk[0]:chunk[1]], chunk[2], ACT.Identity,
                                     bias=biases[:, layer:layer + 1]).then_inc(went, 1)

            def spread_rel(L, p, quads=range(QG)):
                if quads[0] == 0:
                    act.wait_ge(L["pick_made"], p * QG + SEED)
                for c in quads:
                    act.wait_ge(L["t_made"], p * QG + (c + 1 + SEED))
                    nc.scalar.copy(rel_T[:, c * QUAD:(c + 1) * QUAD, :].rearrange("r t e -> r (t e)"),
                                   bank(T_BANK, QUAD * P)).then_inc(L["t_evac"], 1)

            act.wait_ge(small_in, 64)
            act.wait_ge(rounds_ready, 2)
            rounds = act.value_load(nrounds_i[0:1, 0:1], min_val=1, max_val=MAXR)
            qrounds = act.value_load(nrounds_i[0:1, 1:2], min_val=1, max_val=MAXR)
            with act.Fori(0, qrounds) as k:
                for c in range(NCH):
                    at = min(c * BANK, N - BANK)
                    root_to_out(0, (at, at + BANK, bank(AUX_BANK)), root_made, root_out, k * NCH + (c + 1))
            act.wait_ge(root_out, qrounds * NCH + SEED)
            act.sem_inc(root_done, 1)

            def layer(L, first):
                width, in_loop, rest = bodies(L)
                with act.Fori(0, rounds) as k:
                    if first:
                        spread_rel(L, k * NG)
                        spread_rel(L, k * NG + 1)

                    def body(i, last):
                        for u in range(rest if last else width):
                            g = k * NG + i * width + u
                            ahead = first and not (last and u >= rest - 2)
                            for j in range(G // 2):
                                if ahead and j == T_AT:
                                    spread_rel(L, g + 2, range(1))
                                act.wait_ge(L["z_made"], g * (G // 2) + (j + 1))
                                n = min(2, REAL - 2 * j) if last and u == rest - 1 else 2
                                nc.scalar.copy(
                                    z_sb[:, :, 2 * j:2 * j + n, :].rearrange("h r t n -> h t r n"),
                                    bank(Z_BANK + j % Z_BANKS, n * R * WIN).rearrange("h (t r n) -> h t r n", t=n, r=R),
                                ).then_inc(L["z_evac"], 1)
                            if ahead:
                                spread_rel(L, g + 2, range(1, QG))
                            if last:
                                stage(L, u, u * G)
                            elif u < rest:
                                stage(L, u, i * (width * G) + (width + u) * G)
                            else:
                                stage(L, u, ((i + 1) % in_loop) * (width * G) + u * G)

                    with act.Fori(0, in_loop) as i:
                        body(i, False)
                    body(in_loop, True)

            layer(L1, True)
            for q in range(0, JQ, 2):
                nj = min(4, NJ - 4 * q)
                act.wait_ge(h1_turned, q + 1)
                nc.scalar.activation(rows[0:NP, 4 * q:4 * q + nj, :].rearrange("p j d -> p (j d)"),
                                     bank(q % 4, nj * D, NP), ACT.Relu).then_inc(h1_act, 1)
            for u in range(RING):
                stage(L2, u, u * G)
            for c in range(NCH):
                at = c * BANK
                n = min(BANK, N - at)
                root_to_out(1, (at, at + n, bank(c % 4, n)), root2_made, root2_out, c + 1)
            layer(L2, False)

        @block.vector
        def _(dve):
            dve.sem_inc(q_added, SEED)
            for s in [L[n] for L in (L1, L2) for n in ("added", "s_made")]:
                dve.sem_inc(s, SEED)
            dve.sem_inc(L1["node_c_made"], SEED_C)
            nc.vector.memset(dst_i[:, CH - 1, :], 0).then_inc(pads_set, 1)
            nc.vector.memset(src_i[:, CH - 1, :], 0).then_inc(pads_set, 1)
            nc.vector.memset(rel_i[:, CH - 1, :], -1).then_inc(pads_set, 1)
            nc.vector.memset(out_T[:, N:COLS], 0.0).then_inc(tail_zero, 1)
            nc.vector.memset(counts[:, 0:QCOLS // 2], 0.0).then_inc(tail_zero, 1)
            for c in range(NLN):
                j = slice(c * LNC, (c + 1) * LNC)
                if c == NLN - 1:
                    dve.wait_ge(src_in, 48)
                    nc.vector.tensor_copy(src_f, src_i).then_inc(lists_f, 1)
                    dve.wait_ge(rel_in, 48)
                    nc.vector.tensor_copy(rel_f, rel_i).then_inc(lists_f, 1)
                dve.wait_ge(x_in[c], 16)
                for jj in range(c * LNC, (c + 1) * LNC):
                    last = nc.vector.bn_stats(stats[0:NP, jj, :], rows[0:NP, jj, :])
                last.then_inc(ln_stats, 1)
                dve.wait_ge(ln_stats, c + 1)
                for jj in range(c * LNC, (c + 1) * LNC):
                    last = nc.vector.bn_aggr(meanvar[0:NP, jj, :], stats[0:NP, jj, :])
                last.then_inc(ln_aggr, 1)
                dve.wait_ge(ln_aggr, c + 1)
                nc.vector.tensor_scalar(std[0:NP, j], meanvar[0:NP, j, 1], EPS, None, ALU.add).then_inc(ln_var, 1)
                dve.wait_ge(ln_std, c + 1)
                nc.vector.reciprocal(rstd[0:NP, j], std[0:NP, j]).then_inc(ln_rstd, 1)
                dve.wait_ge(ln_rstd, c + 1)
                nc.vector.scalar_tensor_tensor(out=shift[0:NP, j], in0=meanvar[0:NP, j, 0], scalar=-1.0,
                                               in1=rstd[0:NP, j], op0=ALU.mult, op1=ALU.mult).then_inc(ln_scale, 1)
            dve.wait_ge(dst_in, 96)
            nc.vector.tensor_copy(dst_f, dst_i).then_inc(prep, 1)
            dve.wait_ge(prep, 1)
            nc.vector.tensor_reduce(dmin[:], dst_f, AX.X, ALU.min).then_inc(prep, 1)
            nc.vector.tensor_reduce(dmax[:], dst_f, AX.X, ALU.max).then_inc(prep, 1)
            dve.wait_ge(prep, 3)
            nc.vector.tensor_tensor(tile_span[:], dmax[:], dmin[:], ALU.subtract).then_inc(prep, 1)
            dve.wait_ge(prep, 4)
            nc.vector.tensor_reduce(part_span[:], tile_span[:], AX.X, ALU.max).then_inc(prep, 1)
            quads = lambda a: a.rearrange("o (q t) -> o q t", t=QUAD)
            dve.wait_ge(turned, 3)
            nc.vector.tensor_reduce(spans[:, 0:1], ps[0:1, 6 * BANK:6 * BANK + P], AX.X, ALU.max)\
                .then_inc(round_1, 1)
            dve.wait_ge(consts, 4)
            dve.wait_ge(round_1, 1)
            nc.vector.tensor_scalar(round_on, round_no, float(WIN), spans[:, 0:1], ALU.mult,
                                    ALU.is_le).then_inc(round_1, 1)
            dve.wait_ge(round_1, 2)
            nc.vector.tensor_reduce(nrounds_f[:, 0:1], round_on, AX.X, ALU.add).then_inc(round_1, 1)
            dve.wait_ge(round_1, 3)
            nc.vector.tensor_copy(nrounds_i[:, 0:1], nrounds_f[:, 0:1]).then_inc(rounds_ready, 1)
            dve.wait_ge(turned, 4)
            nc.vector.tensor_copy(base_f[:], ps[0:1, 4 * BANK:4 * BANK + NT]).then_inc(base_out, 1)
            nc.vector.tensor_reduce(qmin, quads(ps[0:1, 4 * BANK:4 * BANK + NT]), AX.X, ALU.min).then_inc(base_out, 1)
            dve.wait_ge(base_out, 2)
            nc.vector.tensor_tensor(quads(delta), quads(base_f[:]), qmin.unsqueeze(2).to_broadcast([1, NQ, QUAD]),
                                    ALU.subtract).then_inc(delta_ready, 1)
            dve.wait_ge(turned, 5)
            nc.vector.tensor_reduce(qmax, quads(ps[0:1, 0:NT]), AX.X, ALU.max).then_inc(base_out, 1)
            dve.wait_ge(base_out, 3)
            nc.vector.tensor_tensor(qmax, qmax, qmin, ALU.subtract).then_inc(base_out, 1)
            dve.wait_ge(base_out, 4)
            nc.vector.tensor_reduce(spans[:, 1:2], qmax, AX.X, ALU.max).then_inc(base_out, 1)
            dve.wait_ge(base_out, 5)
            nc.vector.tensor_scalar(round_on_q, round_no[:, 0:QMAXR], float(QWIN), spans[:, 1:2], ALU.mult,
                                    ALU.is_le).then_inc(base_out, 1)
            dve.wait_ge(base_out, 6)
            nc.vector.tensor_reduce(nrounds_f[:, 1:2], round_on_q, AX.X, ALU.add).then_inc(base_out, 1)
            dve.wait_ge(base_out, 7)
            nc.vector.tensor_copy(nrounds_i[:, 1:2], nrounds_f[:, 1:2]).then_inc(rounds_ready, 1)
            dve.wait_ge(delta_spread, 1)
            dve.wait_ge(row_out, 1)
            nc.vector.tensor_tensor(dlq_tab[:], dl_tab[:], bank(4, NT), ALU.add).then_inc(base_out, 1)
            dve.wait_ge(base_out, 8)
            nc.vector.tensor_copy(dlq_b[:], dlq_tab[:]).then_inc(q_base, 1)
            nc.vector.tensor_scalar(qbase_i, qmin, float(QCOLS - QWIN), None, ALU.min).then_inc(q_base, 1)
            dve.wait_ge(rounds_ready, 2)
            rounds = dve.value_load(nrounds_i[0:1, 0:1], min_val=1, max_val=MAXR)
            qrounds = dve.value_load(nrounds_i[0:1, 1:2], min_val=1, max_val=MAXR)
            dve.wait_ge(tabs, 2)

            def hots_of(hot, b, table, col, width):
                return nc.vector.tensor_tensor(hot[:, b, 0:width, :], iota_b[:, 0:width, :],
                                               table[:, ds(col, G)].unsqueeze(1).to_broadcast([P, width, G]),
                                               ALU.is_equal)

            def layer_steps(L, first):
                nc.vector.memset(win_at[:], 0.0).then_inc(L["base_next"], 1)

                def place_windows(n):
                    dve.wait_ge(L["base_next"], n)
                    nc.vector.tensor_scalar(dl_b[:], dl_tab[:], win_at[:], None, ALU.subtract)
                    nc.vector.tensor_scalar(base_i[:], base_f[:], win_at[0:1, :], float(COLS - WIN), ALU.add, ALU.min)\
                        .then_inc(L["base_ready"], 1)

                place_windows(1)

                def hots(p, b, col):
                    hots_of(hot_node, b, dl_b, col, WIN)
                    hots_of(hot_rel, b, rel_b, col, RELP if first else R).then_inc(L["hot_made"], 1)

                def copy_hots(p, b):
                    dve.wait_ge(L["hot_made"], p + 1)
                    dve.wait_ge(L["t_made"], p * QG + SEED)
                    nc.vector.tensor_copy(hot_rel_4[:], hot_rel[:, b, :, :].unsqueeze(1)
                                          .to_broadcast([P, QG, RELP, G])).then_inc(L["hot_4_made"], 1)

                def weighted(p, b, col, before):
                    if first:
                        dve.wait_ge(L["pick_made"], p * QG + (QG + SEED))
                        nc.vector.tensor_tensor(node_c[:], hot_node[:, b, :, :].rearrange("p n t -> p t n")
                                                .unsqueeze(3).to_broadcast([P, G, WIN, 2]),
                                                bank(PICK_BANK + b, G * WIN * 2)
                                                .rearrange("p (t n s) -> p t n s", n=WIN, s=2),
                                                ALU.mult).then_inc(L["node_c_made"], 1)
                        dve.wait_ge(L["node_c_made"], p + (1 + SEED_C))
                        nc.vector.tensor_reduce(count_part[:], node_c[:].rearrange("p t n s -> p t (n s)"), AX.X,
                                                ALU.add).then_inc(L["count_sum"], 1)
                        dve.wait_ge(L["count_sum"], p + 1)
                        nc.vector.tensor_tensor(count_tab[:, ds(col, G)], count_tab[:, ds(col, G)], count_part[:],
                                                ALU.add).then_inc(L["count_added"], 1)
                        dve.wait_ge(L["count_added"], p + 1)
                        nc.vector.tensor_scalar(count_or_1[:], count_tab[:, ds(col, G)], 1.0, None, ALU.max)\
                            .then_inc(L["count_max"], 1)
                        dve.wait_ge(L["count_max"], p + 1)
                        nc.vector.reciprocal(w_tab[:, ds(col, G)], count_or_1[:]).then_inc(L["w_made"], 1)
                        dve.wait_ge(L["w_made"], p + 1)
                    else:
                        dve.wait_ge(L["hot_made"], p + 1)
                    nc.vector.tensor_tensor(node_w[:], hot_node[:, b, :, :],
                                            w_tab[:, ds(col, G)].unsqueeze(1).to_broadcast([P, WIN, G]),
                                            ALU.mult).then_inc(L["node_w_made"], 1)
                    dve.wait_ge(L["node_w_made"], p + 1)
                    for h in range(2):
                        if before is not None:
                            dve.wait_ge(L["z_made"], before * (G // 2) + (h + 1) * (G // 4))
                        t = slice(h * G // 2, (h + 1) * G // 2)
                        nc.vector.tensor_tensor(
                            onehot_w[:, t, :, :],
                            hot_rel[:, b, 0:R, t].rearrange("p r t -> p t r").unsqueeze(3)
                            .to_broadcast([P, G // 2, R, WIN]),
                            node_w[:, :, t].rearrange("p n t -> p t n").unsqueeze(2).to_broadcast([P, G // 2, R, WIN]),
                            ALU.mult).then_inc(L["s_made"], 1)

                return place_windows, hots, copy_hots, weighted

            l1_steps = layer_steps(L1, True)
            dve.wait_ge(L1["base_ready"], 1)
            _, hots_1, copy_hots_1, _ = l1_steps
            hots_1(0, 0, 0)
            hots_1(1, 1, G)
            copy_hots_1(0, 0)

            def quad_hots(b, col):
                hots_of(hot_quad_rel, b, rel_b, col, R)
                hots_of(hot_quad, b, dlq_b, col, QWIN).then_inc(q_hot, 1)

            with dve.Fori(0, qrounds) as k:
                dve.wait_ge(q_base, k * 2 + 2)
                quad_hots(0, 0)
                quad_hots(1, G)

                def count_body(i, last):
                    dve.wait_ge(tail_zero, 3)
                    _, at = nc.values_load_multi_w_load_instructions(
                        qbase_i[0:1, ds(i * (QB * QG), QB * QG)], engines=[mybir.EngineType.DVE],
                        min_val=0, max_val=QCOLS - QWIN,
                        skip_runtime_bounds_check_because="the row was clamped to its bounds when it was written")
                    for u in range(QB):
                        g = k * NG + i * QB + u
                        if not (last and u >= QB - 2):
                            quad_hots((u + 2) % QB, i * (QB * G) + (u + 2) * G)
                        dve.wait_ge(q_added, g * QG + SEED)
                        dve.wait_ge(q_counted, g + 1)
                        for c in range(QG):
                            nc.vector.tensor_tensor(
                                counts[c * RELP:c * RELP + R, ds(at[u * QG + c], QWIN)],
                                counts[c * RELP:c * RELP + R, ds(at[u * QG + c], QWIN)],
                                ps[c * RELP:c * RELP + R, u * BANK:u * BANK + QWIN],
                                ALU.add).then_inc(q_added, 1)

                with dve.Fori(0, NI - 1) as i:
                    count_body(i, False)
                count_body(NI - 1, True)
                with dve.If_lt(dve.to_reg(k + 1), dve.to_reg(qrounds)):
                    nc.vector.tensor_scalar(dlq_tab[:], dlq_tab[:], float(-QWIN), None, ALU.add).then_inc(q_next, 1)
                    nc.vector.tensor_scalar(qmin, qmin, float(QWIN), None, ALU.add).then_inc(q_next, 1)
                    dve.wait_ge(q_next, k * 2 + 2)
                    nc.vector.tensor_copy(dlq_b[:], dlq_tab[:]).then_inc(q_base, 1)
                    nc.vector.tensor_scalar(qbase_i, qmin, float(QCOLS - QWIN), None, ALU.min).then_inc(q_base, 1)
            dve.wait_ge(q_added, qrounds * (NG * QG) + SEED)
            dve.wait_ge(q_base, qrounds * 2)
            nc.vector.tensor_tensor(count_lo, counts[:], count_hi, ALU.subtract).then_inc(counts_made, 1)
            nc.vector.memset(count_tab[:], 0.0).then_inc(tab_zero, 1)
            dve.wait_ge(tab_zero, 1)

            def layer(L, first, steps):
                place_windows, hots, copy_hots, weighted = steps
                width, in_loop, rest = bodies(L)
                with dve.Fori(0, rounds) as k:
                    if first:
                        copy_hots(k * NG + 1, 1)
                    else:
                        dve.wait_ge(L["base_ready"], k + 1)
                        dve.wait_ge(L["s_made"], k * (2 * NG) + SEED)
                        hots(k * NG, 0, 0)
                        hots(k * NG + 1, 1, G)
                    weighted(k * NG, 0, 0, None)
                    dve.wait_ge(L["s_made"], k * (2 * NG) + (2 + SEED))
                    hots(k * NG + 2, 0, 2 * G)
                    if first:
                        copy_hots(k * NG + 2, 0)

                    def body(i, last):
                        for u in range(rest if last else width):
                            g = k * NG + i * width + u
                            col = i * (width * G) + u * G
                            if not (last and u == rest - 1):
                                weighted(g + 1, (u + 1) % 2, col + G, g)
                            if not (last and u >= rest - 3):
                                dve.wait_ge(L["s_made"], g * 2 + (4 + SEED))
                                hots(g + 3, (u + 1) % 2, col + 3 * G)
                                if first:
                                    copy_hots(g + 3, (u + 1) % 2)
                            dve.wait_ge(tail_zero, 3)
                            _, at = nc.values_load_multi_w_load_instructions(
                                base_i[0:1, ds(col, G)], engines=[mybir.EngineType.DVE],
                                min_val=0, max_val=COLS - WIN,
                                skip_runtime_bounds_check_because="the row was clamped to its bounds when written")
                            final = last and u == rest - 1
                            if not final:
                                dve.wait_ge(L["rel_made"], g + 1)
                            for t in range(REAL if final else G):
                                b = (T_BANK, PICK_BANK)[t * 2 // G] if final else REL_BANK
                                if final and t == 0:
                                    dve.wait_ge(L["rel_first"], k + 1)
                                if final and t == G // 2:
                                    dve.wait_ge(L["rel_made"], g + 1)
                                dve.wait_ge(L["added"], g * G + (t + SEED))
                                nc.vector.tensor_tensor(
                                    out_T[:, ds(at[t], WIN)], out_T[:, ds(at[t], WIN)],
                                    bank(b)[:, t * WIN:(t + 1) * WIN],
                                    ALU.add).then_inc(L["added"], 1 + G - REAL if final and t == REAL - 1 else 1)

                    with dve.Fori(0, in_loop) as i:
                        body(i, False)
                    body(in_loop, True)
                    with dve.If_lt(dve.to_reg(k + 1), dve.to_reg(rounds)):
                        nc.vector.tensor_scalar(win_at[:], win_at[:], float(WIN), None, ALU.add)\
                            .then_inc(L["base_next"], 1)
                        place_windows(k + 2)
                        if first:
                            dve.wait_ge(L["base_ready"], k + 2)
                            dve.wait_ge(L["s_made"], (k + 1) * (2 * NG) + SEED)
                            hots(k * NG + NG, 0, 0)
                            hots(k * NG + NG + 1, 1, G)
                            copy_hots(k * NG + NG, 0)

            dve.wait_ge(root_done, 1)
            layer(L1, True, l1_steps)
            for q in range(1, JQ, 2):
                nj = min(4, NJ - 4 * q)
                dve.wait_ge(h1_turned, q + 1)
                nc.vector.tensor_scalar(rows[0:NP, 4 * q:4 * q + nj, :].rearrange("p j d -> p (j d)"),
                                        bank(q % 4, nj * D, NP), 0.0, None, ALU.max).then_inc(h1_dve, 1)
            dve.wait_ge(L1["added"], rounds * (NG * G) + SEED)
            nc.vector.tensor_scalar(h_T[:], out_T[:, 0:N], 0.0, None, ALU.max).then_inc(h1T_made, 1)
            dve.wait_ge(root2_out, NCH)
            layer(L2, False, layer_steps(L2, False))
            dve.wait_ge(x_again, 16)
            for q in range(JQ):
                nj = min(4, NJ - 4 * q)
                r = rows[0:NP, 4 * q:4 * q + nj, :].rearrange("p j d -> p (j d)")
                dve.wait_ge(y_turned, q + 1)
                nc.vector.tensor_tensor(r, r, bank(q % 4, nj * D, NP), ALU.add).then_inc(y_made, 1)

        @block.tensor
        def _(pe):
            pe.sem_inc(L1["pick_made"], SEED)
            pe.sem_inc(L1["t_made"], SEED)
            pe.wait_ge(ident_ready, 2)

            def turn_list(a, s, need, b):
                pe.wait_ge(s, need)
                for c in range(CH):
                    w = min(P, NT - c * P)
                    last = nc.tensor.transpose(ps[:, b * BANK + c * P:b * BANK + c * P + w], a[0:w, c, :],
                                               ident[0:w, 0:w])
                last.then_inc(turned, 1)

            turn_list(src_f, lists_f, 1, 0)
            turn_list(rel_f, lists_f, 2, 2)

            def row_of(col, b):
                for c in range(CH):
                    last = nc.tensor.transpose(ps[0:1, b * BANK + c * P:b * BANK + (c + 1) * P], col[:, c:c + 1],
                                               ident[:])
                last.then_inc(turned, 1)

            def turn_h(q):
                nj = min(4, NJ - 4 * q)
                pe.wait_ge(ln_act, (4 * q + nj - 1) // LNC + 1)
                pe.wait_ge(ln_pool, (4 * q + nj - 1) // LNC + 1)
                if q >= 2:
                    pe.wait_ge(hT_made, q - 1)
                for j in range(nj):
                    last = nc.tensor.transpose(bank(2 + q % 2, 4 * NP)[:, j * NP:(j + 1) * NP],
                                               rows[0:NP, 4 * q + j, :], ident[0:NP, 0:NP])
                last.then_inc(hT_turned, 1)

            pe.wait_ge(prep, 5)
            nc.tensor.transpose(ps[0:1, 6 * BANK:6 * BANK + P], part_span[:], ident[:]).then_inc(turned, 1)
            row_of(dmin, 4)
            pe.wait_ge(tabs, 1)
            row_of(dmax, 0)
            pe.wait_ge(round_1, 1)
            turn_list(dl_f, dl_ready, 1, 6)
            pe.wait_ge(tabs, 2)
            for q in range(HT_EARLY):
                turn_h(q)
            pe.wait_ge(consts, 4)
            pe.wait_ge(delta_ready, 1)
            for c in range(0, NT, BANK):
                n = min(BANK, NT - c)
                last = nc.tensor.matmul(bank(4 + c // BANK, n), ones, delta[:, c:c + n], start=True, stop=True)
            last.then_inc(delta_spread, 1)
            for q in range(HT_EARLY, JQ):
                turn_h(q)
            pe.wait_ge(rounds_ready, 2)
            rounds = pe.value_load(nrounds_i[0:1, 0:1], min_val=1, max_val=MAXR)
            qrounds = pe.value_load(nrounds_i[0:1, 1:2], min_val=1, max_val=MAXR)
            pe.wait_ge(row_out, 1)

            def rel_turn(L, p, c):
                if c == 0:
                    pe.wait_ge(L["hot_4_made"], p + 1)
                pe.wait_ge(L["t_evac"], p * QG + (c + SEED))
                for t in range(QUAD):
                    hot = hot_rel_4[:, :, :, c * QUAD + t].rearrange("p q r -> p (q r)")
                    last = nc.tensor.matmul(bank(T_BANK)[:, t * P:(t + 1) * P], hot, ident_b[:], start=True,
                                            stop=True)
                last.then_inc(L["t_made"], 1)

            pe.wait_ge(small_in, 64)
            pe.wait_ge(hT_made, JQ)
            with pe.Fori(0, qrounds) as k:
                def count_body(i, last_body):
                    for u in range(QB):
                        g = k * NG + i * QB + u
                        pe.wait_ge(q_hot, g + 1)
                        for t in range(G):
                            c = t // QUAD
                            last = nc.tensor.matmul(
                                ps[c * RELP:c * RELP + R, u * BANK:u * BANK + QWIN],
                                hot_quad_rel[:, u, :, t], hot_quad[:, u, :, t], start=t % QUAD == 0,
                                stop=t % QUAD == QUAD - 1)
                        last.then_inc(q_counted, 1)
                    pe.wait_ge(root_out, k * NCH + (i + SEED))
                    h_cols = h_T[:, N - BANK:N] if last_body else h_T[:, ds(i * BANK, BANK)]
                    nc.tensor.matmul(bank(AUX_BANK), roots[:, 0, :], h_cols, start=True,
                                     stop=True).then_inc(root_made, 1)

                with pe.Fori(0, NI - 1) as i:
                    count_body(i, False)
                count_body(NI - 1, True)
            pe.wait_ge(w_in, 16 * R)
            pe.wait_ge(root_done, 1)

            def pick(L, p, b, c, at):
                if c == 0:
                    pe.wait_ge(L["node_c_made"], p + (SEED_C - 1))
                pe.wait_ge(L["t_evac"], p * QG + (c + 1 + SEED))
                pe.wait_ge(counts_made, 1)
                for t in range(c * QUAD, (c + 1) * QUAD):
                    last = nc.tensor.matmul(bank(PICK_BANK + b)[:, t * 2 * WIN:(t + 1) * 2 * WIN],
                                            rel_T[:, t, :], halves[:, ds(at[t] * 2, 2 * WIN)], start=True, stop=True)
                last.then_inc(L["pick_made"], 1)

            def windows(col):
                return nc.values_load_multi_w_load_instructions(
                    base_i[0:1, ds(col, G)], engines=[mybir.EngineType.PE], min_val=0, max_val=COLS - WIN,
                    skip_runtime_bounds_check_because="the row was clamped to its bounds when it was written")[1]

            def layer(L, first):
                width, in_loop, rest = bodies(L)
                with pe.Fori(0, rounds) as k:
                    if first:
                        for c in range(QG):
                            rel_turn(L, k * NG, c)
                        for p in range(2):
                            at = windows(p * G)
                            for c in range(QG):
                                if p > 0:
                                    rel_turn(L, k * NG + p, c)
                                pick(L, k * NG + p, p, c, at)

                    def body(i, last):
                        for u in range(rest if last else width):
                            g = k * NG + i * width + u
                            ahead = first and not (last and u >= rest - 2)
                            if ahead:
                                at = windows(i * (width * G) + (u + 2) * G)
                            final = last and u == rest - 1
                            in_quads = last and u >= rest - 2
                            if not in_quads:
                                pe.wait_ge(L["gathered"][u], fills_of_slot(L, u, k, i) * (16 * G))

                            def relations(b, tiles, made):
                                for r in range(R):
                                    mm = nc.tensor.matmul(
                                        bank(b)[:, tiles.start * WIN:tiles.stop * WIN], wrel[:, r, :],
                                        z_sb[:, r, tiles, :].rearrange("h t n -> h (t n)"),
                                        start=(r == 0), stop=(r == R - 1))
                                    if ahead and r in PICKS_AT:
                                        c = PICKS_AT.index(r) + 1
                                        pick(L, g + 2, u % 2, c, at)
                                        if c < QG - 1:
                                            rel_turn(L, g + 2, c + 1)
                                mm.then_inc(made, 1)

                            for j in range(G // 2):
                                if ahead and j == T_AT:
                                    rel_turn(L, g + 2, 0)
                                if j % (G // 4) == 0:
                                    pe.wait_ge(L["s_made"], g * 2 + (j // (G // 4) + 1 + SEED))
                                if in_quads and j % 2 == 0:
                                    pe.wait_ge(L["last_quad"][u - rest + 2][j // 2],
                                               (k + 1) * (16 * len(last_quads[u - rest + 2][j // 2])))
                                pe.wait_ge(L["z_evac"], g * (G // 2) + (j + 1))
                                for t in range(2 * j, min(2 * j + 2, REAL) if final else 2 * j + 2):
                                    mm = nc.tensor.matmul(
                                        bank(Z_BANK + j % Z_BANKS, 2 * R * WIN)[:, t % 2 * R * WIN:(t % 2 + 1) * R * WIN],
                                        L["slots"][u][:, t, :], onehot_w[:, t, :, :].rearrange("p r n -> p (r n)"),
                                        start=True, stop=True)
                                mm.then_inc(L["z_made"], 1)
                                if final and j == G // 4 - 1:
                                    pe.wait_ge(L["z_evac"], g * (G // 2) + (G // 4 + Z_BANKS))
                                    relations(T_BANK, slice(0, G // 2), L["rel_first"])
                            if ahead:
                                pick(L, g + 2, u % 2, 0, at)
                                rel_turn(L, g + 2, 1)
                            pe.wait_ge(L["z_evac"], g * (G // 2) + (G // 2 + Z_BANKS))
                            if final:
                                relations(PICK_BANK, slice(G // 2, REAL), L["rel_made"])
                            else:
                                pe.wait_ge(L["added"], g * G + SEED)
                                relations(REL_BANK, slice(0, G), L["rel_made"])

                    with pe.Fori(0, in_loop) as i:
                        body(i, False)
                    body(in_loop, True)

            def out_rows(L, turned_s, ready):
                pe.wait_ge(L["added"], rounds * (NG * G) + SEED)
                for q in range(JQ):
                    nj = min(4, NJ - 4 * q)
                    if q >= 4:
                        ready(q)
                    for j in range(nj):
                        mm = nc.tensor.transpose(bank(q % 4, BANK, NP)[:, j * D:(j + 1) * D],
                                                 node_cols(out_T, 4 * q + j, 1).rearrange("h j p -> h (j p)"),
                                                 ident[:])
                    mm.then_inc(turned_s, 1)

            layer(L1, True)
            out_rows(L1, h1_turned, lambda q: pe.wait_ge(h1_dve if q % 2 else h1_act, (q - 4) // 2 + 1))
            pe.wait_ge(h1_act, (JQ + 1) // 2)
            pe.wait_ge(h1_dve, JQ // 2)
            pe.wait_ge(h1T_made, 1)
            for c in range(NCH):
                n = min(BANK, N - c * BANK)
                if c >= 4:
                    pe.wait_ge(root2_out, c - 3)
                nc.tensor.matmul(bank(c % 4, n), roots[:, 1, :], h_T[:, c * BANK:c * BANK + n], start=True,
                                 stop=True).then_inc(root2_made, 1)
            pe.wait_ge(w2_in, 16 * R)
            pe.wait_ge(root2_out, NCH)
            layer(L2, False)
            out_rows(L2, y_turned, lambda q: pe.wait_ge(y_made, q - 3))


_INS = ["x", "src", "dst", "edge_type_16", "L0_gnn_W1", "L0_gnn_root1", "L0_gnn_b1", "L0_gnn_W2", "L0_gnn_root2",
        "L0_gnn_b2"]


def kernel(**inputs):
    import numpy as _np
    import concourse.bacc as _bacc
    from concourse import mybir as _mybir
    from concourse.bass_utils import run_bass_kernel_spmd as _run

    nc = _bacc.Bacc("TRN2", target_bir_lowering=False, num_devices=1)
    arrays, args = {}, []
    for name in _INS:
        a = _np.ascontiguousarray(inputs[name])
        arrays[f"in_{name}_dram"] = a
        args.append(nc.dram_tensor(f"in_{name}_dram", a.shape, _mybir.dt.from_np(a.dtype), kind="ExternalInput").ap())
    shape = inputs["x"].shape
    args.append(nc.dram_tensor("out_0_dram", shape, _mybir.dt.float32, kind="ExternalOutput").ap())
    rgcn_kernel(nc, *args)
    r = _run(nc, [arrays], core_ids=[0])
    return r.results[0]["out_0_dram"]
```
